# Optimizing a Trainium2 kernel written in Bass

```python
import numpy as np
import jax
import jax.numpy as jnp

def _softmax(x, axis=-1):
    return jax.nn.softmax(x, axis=axis)

def _gelu(x):
    return jax.nn.gelu(x, approximate=True)

def _silu(x):
    return jax.nn.silu(x)

def _sigmoid(x):
    return jax.nn.sigmoid(x)

def _layernorm(x, axis=-1, eps=1e-05):
    m = jnp.mean(x, axis=axis, keepdims=True)
    v = jnp.var(x, axis=axis, keepdims=True)
    return (x - m) / jnp.sqrt(v + eps)

def _scatter_add(tgt, idx, src, axis=0):
    return tgt.at[idx].add(src)

def _segment_sum(src, seg, n):
    return jax.ops.segment_sum(src, seg, n)
kernel_name = 'mk_prb_d1_jaxref_r4_eb16c9'

def setup_inputs(seed: int=0):
    np.random.seed(seed)
    _w = jnp.asarray

    def _L0_attn_setup():
        import jax, jax.numpy as jnp
        import numpy as np
        D_MODEL = 256
        STATE_DIM = 64
        BATCH = 4
        SEQ_LEN = 1024
        key = jax.random.key(seed)
        k_u, k_B, k_C = jax.random.split(key, 3)
        u = jax.random.normal(k_u, (BATCH, SEQ_LEN, D_MODEL), dtype=jnp.float32)
        log_lambda = jnp.linspace(2.94, 4.6, STATE_DIM, dtype=jnp.float32)
        B_w = jax.random.normal(k_B, (STATE_DIM, D_MODEL), dtype=jnp.float32) / np.sqrt(D_MODEL)
        C_w = jax.random.normal(k_C, (D_MODEL, STATE_DIM), dtype=jnp.float32) / np.sqrt(STATE_DIM)
        D = jnp.ones((D_MODEL,), dtype=jnp.float32)
        return {'u': u, 'log_lambda': log_lambda, 'B_w': B_w, 'C_w': C_w, 'D': D}
    _L0_attn_in = _L0_attn_setup()

    def _L0_ffn_setup():
        import jax, jax.numpy as jnp
        import numpy as np
        B, S, D, E, F = (4, 512, 256, 8, 1024)
        MIN_CAPACITY = 4

        def _make_waff():
            g = D // E
            scale = E / D
            w = np.zeros((E, D), np.float32)
            for i in range(E):
                w[i, i * g:(i + 1) * g] = scale
            return jnp.asarray(w)
        key = jax.random.key(seed)
        ks = jax.random.split(key, 6)
        inputs = jax.random.normal(ks[0], (B, S, D), dtype=jnp.float32)
        W1 = jax.random.normal(ks[1], (E, D, F), dtype=jnp.float32) * (1.0 / np.sqrt(D))
        b1 = jnp.zeros((E, F), dtype=jnp.float32)
        W2 = jax.random.normal(ks[2], (E, F, D), dtype=jnp.float32) * (1.0 / np.sqrt(F))
        b2 = jnp.zeros((E, D), dtype=jnp.float32)
        return {'inputs': inputs, 'waff': _make_waff(), 'W1': W1, 'b1': b1, 'W2': W2, 'b2': b2, 'affinity_threshold': jnp.float32(0.5)}
    _L0_ffn_in = _L0_ffn_setup()
    _d = {'L0_attn_u': _L0_attn_in['u'], 'L0_attn_log_lambda': _L0_attn_in['log_lambda'], 'L0_attn_B_w': _L0_attn_in['B_w'], 'L0_attn_C_w': _L0_attn_in['C_w'], 'L0_attn_D': _L0_attn_in['D'], 'L0_ffn_waff': _L0_ffn_in['waff'], 'L0_ffn_W1': _L0_ffn_in['W1'], 'L0_ffn_b1': _L0_ffn_in['b1'], 'L0_ffn_W2': _L0_ffn_in['W2'], 'L0_ffn_b2': _L0_ffn_in['b2'], 'L0_ffn_affinity_threshold': _L0_ffn_in['affinity_threshold']}
    _x0 = _d['L0_attn_u']
    _d['L0_attn_u'] = jax.random.normal(jax.random.fold_in(jax.random.key(seed), 1), (16, 512, 256), dtype=_x0.dtype)
    del _x0
    return _d

def reference(L0_attn_u, L0_attn_log_lambda, L0_attn_B_w, L0_attn_C_w, L0_attn_D, L0_ffn_waff, L0_ffn_W1, L0_ffn_b1, L0_ffn_W2, L0_ffn_b2, L0_ffn_affinity_threshold):

    def _L0_attn_ref(u, log_lambda, B_w, C_w, D):
        import jax, jax.numpy as jnp
        import numpy as np
        D_MODEL = 256
        STATE_DIM = 64
        BATCH = 4
        SEQ_LEN = 1024
        batch, seq_len, d = u.shape
        Bu = jnp.einsum('bld,nd->bln', u, B_w)
        lam = jax.nn.sigmoid(log_lambda)
        t = jnp.arange(seq_len, dtype=lam.dtype)
        kernel = lam[None, :] ** t[:, None]
        fft_len = 1
        while fft_len < 2 * seq_len:
            fft_len *= 2
        K_hat = jnp.fft.rfft(kernel, n=fft_len, axis=0)
        Bu_hat = jnp.fft.rfft(Bu, n=fft_len, axis=1)
        h_hat = K_hat[None, :, :] * Bu_hat
        h = jnp.fft.irfft(h_hat, n=fft_len, axis=1)[:, :seq_len, :]
        y = jnp.einsum('bln,dn->bld', h, C_w) + D * u
        return y

    def _L0_ffn_ref(inputs, waff, W1, b1, W2, b2, affinity_threshold):
        import jax, jax.numpy as jnp
        import numpy as np
        B, S, D, E, F = (4, 512, 256, 8, 1024)
        MIN_CAPACITY = 4

        def _make_waff():
            g = D // E
            scale = E / D
            w = np.zeros((E, D), np.float32)
            for i in range(E):
                w[i, i * g:(i + 1) * g] = scale
            return jnp.asarray(w)
        num = jnp.einsum('bsd,ed->bse', inputs, waff)
        x_norm = jnp.linalg.norm(inputs, axis=-1, keepdims=True)
        w_norm = jnp.linalg.norm(waff, axis=-1)
        aff = num / (x_norm * w_norm[None, None, :] + 1e-09)
        router_probs = jax.nn.softmax(aff, axis=-1)
        cap = jnp.floor(S * jax.nn.sigmoid(aff.mean() - affinity_threshold)).astype(jnp.int32)
        cap = jnp.minimum(jnp.maximum(cap, MIN_CAPACITY), S)
        tcr = jax.nn.one_hot(jnp.argmax(router_probs, axis=-1), E, dtype=inputs.dtype)
        order = jnp.argsort(-aff, axis=1)
        ranks = jnp.argsort(order, axis=1)
        ecr = (ranks < cap).astype(inputs.dtype)
        dispatch = tcr * ecr
        masks = jnp.moveaxis(dispatch, -1, 0)

        def body(acc, expert):
            W1e, b1e, W2e, b2e, me = expert
            xi = inputs * me[..., None]
            h = jax.nn.gelu(xi @ W1e + b1e, approximate=False)
            return (acc + (h @ W2e + b2e), None)
        out, _ = jax.lax.scan(body, jnp.zeros_like(inputs), (W1, b1, W2, b2, masks))
        return out
    x = L0_attn_u
    xn = _layernorm(x, axis=-1)
    x = x + _L0_attn_ref(xn, L0_attn_log_lambda, L0_attn_B_w, L0_attn_C_w, L0_attn_D) + _L0_ffn_ref(xn, L0_ffn_waff, L0_ffn_W1, L0_ffn_b1, L0_ffn_W2, L0_ffn_b2, L0_ffn_affinity_threshold)
    return x

_drawn_inputs = setup_inputs


def setup_inputs(seed=0):
    import zlib

    import numpy as np

    out = dict(_drawn_inputs(seed))
    spreads = {'L0_attn_D': (1.0, 0.2), 'L0_ffn_b1': (0.0, 0.302), 'L0_ffn_b2': (0.0, 0.1)}
    factors = {}
    for name, (base, spread) in spreads.items():
        noise = np.random.default_rng([zlib.crc32(name.encode()), seed]).standard_normal(out[name].shape)
        drawn = base * np.exp(spread * noise) if base else spread * noise
        out[name] = jnp.asarray(drawn.astype(out[name].dtype))
    for name, factor in factors.items():
        out[name] = (out[name] * factor).astype(out[name].dtype)
    return out
```

```python
import concourse.bass as bass
from concourse import mybir
from contextlib import ExitStack

F32 = mybir.dt.float32
F16 = mybir.dt.float16
I32 = mybir.dt.int32
ACT = mybir.ActivationFunctionType
ALU = mybir.AluOpType
AX = mybir.AxisListType
RMAX = bass.bass_isa.ReduceOp.max

P = 128


def moe_ssm_kernel(nc, u, log_lambda, B_w, C_w, D_w, waff, W1, b1, W2, b2, threshold, out, xn_dram, base_dram):
    B, S, D = u.shape
    N = B_w.shape[0]
    E, _, F = W1.shape
    Q = S // P
    T = B * Q
    TOKENS = B * S
    K = D // P
    C = F // P
    NT = T + E
    PAIRS = B // 2
    UW = K * F
    assert N == 64 and B * E == P and K * F == C * D and NT % 2 == 0
    EPS = 1e-5
    XS = 2.0 ** 11
    NEAR = -(2.0 ** -25)

    u_q = u.rearrange("b (q p) d -> b p q d", p=P)
    xn_q = xn_dram.rearrange("(b q p) d -> b p q d", p=P, q=Q)
    base_q = base_dram.rearrange("(b q p) d -> b p q d", p=P, q=Q)
    out_rows = out.rearrange("b s d -> (b s) d")
    w1_v = W1.rearrange("e (k p) f -> e p k f", p=P)
    w2_v = W2.rearrange("e (c p) d -> e p c d", p=P)

    with ExitStack() as ctx:
        def sb(name, cols, dt=F32, rows=P):
            return ctx.enter_context(nc.sbuf_tensor(name, [rows, cols], dt))

        def sem(name):
            return ctx.enter_context(nc.semaphore(name))

        def part_(t, off, n):
            return t[:, off:off + n]

        whi = sb("whi", 2 * E * UW, F16)
        wlo = sb("wlo", 2 * E * UW, F16)
        ring = sb("ring", 4 * UW)
        work = sb("work", 10 * Q * D)
        ident = sb("ident", P)
        ones = sb("ones", P)
        iota_f = sb("iota_f", P)
        pcol = sb("pcol", 2)
        bt = sb("bt", K * N)
        wat = sb("wat", K * E)
        ct = sb("ct", D)
        d_bc = sb("d_bc", D)
        c_bc = sb("c_bc", D)
        b1t = sb("b1t", E * C)
        lam = sb("lam", 4)
        small = sb("small", 64)
        lam_c = lam[:, 3:4]
        newt = sb("newt", 2 * Q)
        stats = sb("stats", 2 * Q * 6)
        exp_w = sb("exp_w", 2 * E, I32)
        exp_h = sb("exp_h", E, I32)
        tmp_i = sb("tmp_i", 2 * E, I32)
        wnorm = sb("wnorm", E)
        thr_bc = sb("thr_bc", 1)
        mv_s = sb("mv_s", 2 * 4 * Q)
        rstd_s = sb("rstd_s", 2 * 2 * Q)
        ve_s = sb("ve_s", 2 * 2 * Q)
        ratio_all = sb("ratio_all", T)
        wsum = sb("wsum", 4)
        wmax = sb("wmax", 4)
        scale_w = sb("scale_w", 2 * E)
        inv_in = sb("inv_in", E)
        h_scale = sb("h_scale", E)
        inv_out = sb("inv_out", E)
        idx_x = sb("idx_x", 4, I32)
        idx_b = sb("idx_b", 4, I32)
        bits = sb("bits", 8, I32)
        cnt = sb("cnt", 8)

        mv = [part_(mv_s, n * 4 * Q, 4 * Q) for n in range(2)]
        rstd = [part_(rstd_s, n * 2 * Q, 2 * Q) for n in range(2)]
        ve = [part_(ve_s, n * 2 * Q, 2 * Q) for n in range(2)]
        def part(t, off, n):
            return t[:, off:off + n]
        QD = Q * D
        xb = [part(work, n * QD, QD).rearrange("p (q d) -> p q d", q=Q) for n in range(4)]
        xnb = [part(work, (4 + n) * QD, QD).rearrange("p (q d) -> p q d", q=Q) for n in range(2)]
        xnt = [part(work, (6 + n) * QD, QD).rearrange("p (k s) -> p k s", k=K) for n in range(2)]
        hs = [part(work, 8 * QD + n * S, S) for n in range(2)]
        dxn = part(work, 9 * QD, QD).rearrange("p (q d) -> p q d", q=Q)
        iota_i = part(work, 9 * QD + 3 * D, P).bitcast(I32)
        idx_all = part(work, 9 * QD, NT).bitcast(I32)
        mask_slot = part(work, 9 * QD + NT, NT)
        tile_expert = part(work, 9 * QD + 2 * NT, NT).bitcast(I32)
        gb16 = part(work, 9 * QD + 3 * NT, E * C).bitcast(F16)
        ones16 = part(work, 9 * QD + 2 * D, P // 2).bitcast(F16)
        tri16 = part(work, 9 * QD + 2 * D + P // 2, P // 2).bitcast(F16)
        raw = [part(ring, n * UW, UW) for n in range(4)]
        st_b = dxn.rearrange("p q d -> p (q d)")[0:N, 0:D]
        st_c = hs[0][:, 0:K * 2 * N].rearrange("p (k r n) -> p k r n", k=K, r=2)
        st_w = hs[1][0:E, 0:D]
        st_b1 = dxn.rearrange("p q d -> p (q d)")[0:E * C, D:D + P]
        st_b2 = hs[1][0:E, D:2 * D]
        watsq = dxn.rearrange("p q d -> p (q d)")[:, 2 * D:2 * D + K * E]

        TE = T * E
        aff, a_rows, eq_rows = [part(work, n * TE, TE) for n in range(3)]
        oh16 = part(work, 3 * TE, TE // 2).bitcast(F16)
        o = 3 * TE + TE // 2
        (best, rowmax, pos, hi_f, lo_f, tnum, mtok, xnorm, sq0, sq1, ratio) = [part(work, o + n * T, T) for n in range(11)]
        pos_i, hi_i, lo_i = [part(work, o + (11 + n) * T, T).bitcast(I32) for n in range(3)]
        o += 14 * T
        lo16 = part(work, o, T * P // 2).bitcast(F16).rearrange("p (t l) -> p t l", l=P)
        e16 = part(work, o + T * P // 2, T * NT // 2).bitcast(F16).rearrange("p (t j) -> p t j", j=NT)
        diff, cnt_e, scan_e, pos4, den = [part(work, o + n * TE, TE) for n in range(5)]
        v16 = part(ring, 4 * UW - T * NT, T * NT).bitcast(F16).rearrange("p (r t j) -> p r t j", r=2, j=NT)
        g_bc = part(ring, 0, E * D)
        tcmp = part(ring, E * D, NT * E)
        gelu_b = part(ring, E * D + NT * E, E * C)
        h32 = [part(ring, E * D + n * F, F) for n in range(2)]
        hhi = [part(ring, E * D + 2 * F + n * F, F // 2).bitcast(F16) for n in range(2)]
        hlo = [part(ring, E * D + 2 * F + n * F + F // 2, F // 2).bitcast(F16) for n in range(2)]
        so = 0
        xg = [part(work, n * D, D) for n in range(2)]
        bg = [part(work, (2 + n) * D, D) for n in range(2)]
        og = [part(work, (4 + n) * D, D) for n in range(2)]
        yr = [part(work, (6 + n) * D, D) for n in range(2)]
        xhi = [part(work, 8 * D + n * D, D // 2).bitcast(F16).rearrange("p (k t) -> p k t", k=K) for n in range(2)]
        xlo = [part(work, 8 * D + n * D + D // 2, D // 2).bitcast(F16).rearrange("p (k t) -> p k t", k=K) for n in range(2)]

        def psum(name, cols):
            return ctx.enter_context(nc.psum_tensor(name, [P, cols], F32))
        ps_t = psum("ps_t", 1024)
        ps_bu = psum("ps_bu", 512)
        ps_num = psum("ps_num", 512)
        ps_y = psum("ps_y", 1024)
        ps_s = psum("ps_s", 512)
        ps_g = psum("ps_g", 512)
        ps_h = [ps_t, ps_y]
        ps_x = [ps_s, ps_g]
        ps_o = [ps_bu, ps_num]

        s = {n: sem(n) for n in (
            "params_in", "consts", "pe_const", "dve_const", "act_const",
            "x_in0", "x_in1", "x_in2", "x_in3", "w_in0", "w_in1", "w_in2", "w_in3",
            "stats", "std", "rstd_ok", "xn_ok", "xt_ok", "xt_out", "num_ok", "bu_ok", "scan_ok", "y_ok",
            "dx_ok", "base_ok", "xn_out0", "xn_out1", "base_out0", "base_out1", "base_out2", "base_out3",
            "wsum_ok", "wmax_ok", "wscale_ok", "whi_ok", "wlo_ok",
            "dve_chain", "r_pe", "r_act", "r_dve", "r_pool", "g_pe", "g_dve",
            "oh_pos", "inv_pe", "idx_ok", "m_ok",
            "gx0", "gx1", "gb0", "gb1", "sc0", "sc1", "ix", "ib",
            "f_xt", "f_xhi", "f_xlo", "f_h", "f_gelu", "f_hhi", "f_hlo", "f_y", "f_yr", "f_ym", "f_o",
            "gates", "cleared", "r_dve2", "r_pool2", "newton", "wchain", "ratio_c")}
        block = ctx.enter_context(nc.Block())
        x_in = [s[f"x_in{n}"] for n in range(4)]
        w_in = [s[f"w_in{n}"] for n in range(4)]
        xn_out = [s[f"xn_out{n}"] for n in range(2)]
        base_out = [s[f"base_out{n}"] for n in range(4)]

        def wait(eng, sm, v):
            if not (isinstance(v, int) and v <= 0):
                eng.wait_ge(sm, v)

        PARAMS = 10 * 16

        @block.sync
        def _(sp):
            def load(dst, src):
                sp.dma_start(dst, src).then_inc(s["params_in"], 16)
            load(st_b, B_w)
            load(st_c[:, :, 0, :], C_w.rearrange("(k p) n -> p k n", p=P))
            load(st_c[:, :, 1, :], C_w.rearrange("(k p) n -> p k n", p=P))
            load(st_w, waff)
            load(st_b1, b1.rearrange("e (c f) -> (e c) f", f=P))
            load(st_b2, b2)
            load(lam[0:N, 0:1], log_lambda)
            load(lam[N:2 * N, 0:1], log_lambda)
            load(d_bc[:, :], D_w.partition_broadcast(P))
            load(thr_bc[:, :], threshold.partition_broadcast(P))
            for n in range(4):
                sp.dma_start(xb[n], u_q[n]).then_inc(x_in[n], 16)

            def turn(i, last):
                for pr in range(2):
                    for h in range(2):
                        n = 2 * pr + h
                        b = i * 4 + n
                        if not isinstance(b, int):
                            b = sp.snap(b, min_val=0, max_val=B - 1)
                            v1 = sp.snap(i * 4 + n + 1)
                        else:
                            v1 = i * 4 + n + 1
                        sp.wait_ge(s["xn_ok"], v1)
                        sp.dma_start(xn_q[bass.ds(b, 1)].rearrange("a p q d -> (a p) q d"),
                                     xnb[h]).then_inc(xn_out[h], 16)
                    for h in range(2):
                        n = 2 * pr + h
                        b = i * 4 + n
                        if not isinstance(b, int):
                            b = sp.snap(b, min_val=0, max_val=B - 1)
                            v1 = sp.snap(i * 4 + n + 1)
                            v2 = sp.snap(i * 16 + 16)
                        else:
                            v1 = i * 4 + n + 1
                            v2 = i * 16 + 16
                        sp.wait_ge(s["base_ok"], v1)
                        sp.dma_start(base_q[bass.ds(b, 1)].rearrange("a p q d -> (a p) q d"),
                                     xb[n]).then_inc(base_out[n], 16)
                        if not last:
                            b2_ = sp.snap(i * 4 + (n + 4), min_val=0, max_val=B - 1) if not isinstance(b, int) else b + 4
                            sp.wait_ge(base_out[n], v2)
                            sp.dma_start(xb[n], u_q[bass.ds(b2_, 1)].rearrange("a p q d -> (a p) q d")).then_inc(x_in[n], 16)
            turn(0, False)
            with sp.Fori(1, PAIRS // 2 - 1) as i:
                turn(i, False)
            turn(PAIRS // 2 - 1, True)

        @block.gpsimd
        def _(pool):
            g = nc.gpsimd
            link_n = [0]

            def link(ins):
                link_n[0] += 1
                ins.then_inc(s["r_pool"], 1)
                pool.wait_ge(s["r_pool"], link_n[0])
            link(g.memset(ident[:], 1.0))
            link(g.affine_select(out=ident[:], in_=ident[:], compare_op=ALU.is_equal, fill=0.0, base=0,
                                 pattern=[[-1, P]], channel_multiplier=1))
            link(g.memset(ones[:], 1.0))
            link(g.iota(iota_i[:], [[1, P]], base=0, channel_multiplier=0))
            link(g.tensor_copy(iota_f[:], iota_i[:]))
            link(g.iota(iota_i[:, 0:1], [[0, 1]], base=1, channel_multiplier=1))
            g.tensor_copy(pcol[:, 0:1], iota_i[:, 0:1]).then_inc(s["consts"], 1)
            pool.wait_ge(s["consts"], 1)

            def gate(before):
                wait(pool, s["gates"], before)
                g.tensor_tensor(cnt[:, 5:6], ones[:, 0:1], ones[:, 0:1], ALU.add).then_inc(s["gates"], 1)

            def turn(i):
                for pr in range(2):
                    for h in range(2):
                        n = 2 * pr + h
                        uu = i * 4 + n
                        pool.wait_ge(s["wsum_ok"], i * 4 + (n + 1))
                        gate(i * 4 + n)
                        g.partition_all_reduce(wmax[:, n:n + 1], wsum[:, n:n + 1], P,
                                               RMAX).then_inc(s["wmax_ok"], 1)
                    for h in range(2):
                        n = 2 * pr + h
                        bat = i * 4 + n
                        pool.wait_ge(s["xn_ok"], bat + 1)
                        wait(pool, s["dx_ok"], bat * 2)
                        g.tensor_tensor(dxn, xnb[h], d_bc[:].rearrange("p (a d) -> p a d", a=1).to_broadcast([P, Q, D]),
                                        ALU.mult).then_inc(s["dx_ok"], 1)
                        pool.wait_ge(s["dx_ok"], i * 8 + (2 * n + 1))
                        g.tensor_tensor(xb[n], xb[n], dxn, ALU.add).then_inc(s["dx_ok"], 1)
            pool.wait_ge(s["params_in"], PARAMS)
            pool.wait_ge(s["pe_const"], 4)
            turn(0)
            with pool.Fori(1, PAIRS // 2) as i:
                turn(i)

            gx, gb, sc = [s["gx0"], s["gx1"]], [s["gb0"], s["gb1"]], [s["sc0"], s["sc1"]]
            for n in range(2):
                pool.wait_ge(xn_out[n], 16 * (B // 2))
            for n in range(4):
                pool.wait_ge(base_out[n], 16 * (B // 4))
            link(g.tensor_copy(ones16, ones[:]))
            link(g.iota(iota_i[:, 0:T], [[1, Q], [Q, B]], base=0, channel_multiplier=0))
            link(g.tensor_copy(tnum, iota_i[:, 0:T]))
            g.affine_select(out=tri16, in_=ones16, compare_op=ALU.is_gt, fill=0.0, base=0,
                            pattern=[[1, P]], channel_multiplier=-1).then_inc(s["r_pool2"], 1)
            pool.wait_ge(s["r_dve"], 2)
            g.partition_all_reduce(small[:, 56:64], small[:, 48:56], P, RMAX).then_inc(s["r_pool2"], 1)
            pool.wait_ge(s["idx_ok"], 1)
            for p in range(2):
                g.memset(xg[p], 0.0)
                g.memset(bg[p], 0.0).then_inc(s["cleared"], 1)
            pool.wait_ge(s["cleared"], 2)

            bound = pool.to_reg(TOKENS - 1)

            def is_tile(j):
                return not isinstance(j, int) or 0 <= j < NT

            def step(m, r, gate_no):
                t_out, t_base = m - 5, m - 3
                if is_tile(m):
                    wait(pool, s["f_xt"], m - 1)
                    gate(gate_no)
                    g.tensor_copy(idx_x[:, r:r + 1], idx_all[:, bass.ds(m, 1)]).then_inc(s["ix"], 1)
                    pool.wait_ge(s["ix"], m + 1)
                    gate(gate_no + 1)
                    gate_no = gate_no + 2
                    g.indirect_dma_start(out=xg[r % 2], out_offset=None, in_=xn_dram,
                                         in_offset=bass.IndirectOffsetOnAxis(ap=idx_x[:, r:r + 1], axis=0),
                                         bounds_check=bound, oob_is_err=False).then_inc(gx[r % 2], 16)
                rb = (r + 1) % 4
                if is_tile(t_out):
                    pool.wait_ge(s["f_o"], t_out + 1)
                    gate(gate_no)
                    gate_no = gate_no + 1
                if is_tile(t_base):
                    g.tensor_copy(idx_b[:, rb:rb + 1], idx_all[:, bass.ds(t_base, 1)]).then_inc(s["ib"], 1)
                if is_tile(t_out):
                    ro = (r + 3) % 4
                    g.indirect_dma_start(out=out_rows,
                                         out_offset=bass.IndirectOffsetOnAxis(ap=idx_b[:, ro:ro + 1], axis=0),
                                         in_=og[ro % 2], in_offset=None,
                                         bounds_check=bound, oob_is_err=False).then_inc(sc[ro % 2], 16)
                if is_tile(t_base):
                    pool.wait_ge(s["ib"], t_base + 1)
                    gate(gate_no)
                    gate_no = gate_no + 1
                    g.indirect_dma_start(out=bg[rb % 2], out_offset=None, in_=base_dram,
                                         in_offset=bass.IndirectOffsetOnAxis(ap=idx_b[:, rb:rb + 1], axis=0),
                                         bounds_check=bound, oob_is_err=False).then_inc(gb[rb % 2], 16)
                return gate_no
            gates = B
            for m in range(8):
                gates = step(m, m % 4, gates)
            with pool.Fori(2, NT // 4) as i:
                for r in range(4):
                    step(i * 4 + r, r, i * 16 + (gates - 32 + 4 * r))
            gates += 4 * (NT - 8)
            for m in range(NT, NT + 5):
                gates = step(m, m % 4, gates)
            for p in range(2):
                pool.wait_ge(sc[p], 16 * (NT // 2))

        @block.scalar
        def _(act):
            a = nc.scalar

            def load_w(uu, slot):
                e = uu // 2 if isinstance(uu, int) else None
                return e

            def wload(e, w, slot):
                v = (w1_v if w == 0 else w2_v)[bass.ds(e, 1)].rearrange("a p k f -> (a p) k f")
                dst = raw[slot].rearrange("p (k f) -> p k f", k=K if w == 0 else C)
                act.dma_start(dst, v).then_inc(w_in[slot], 16)
            for n in range(4):
                wload(n // 2, n % 2, n)
            act.wait_ge(s["params_in"], PARAMS)
            a.activation(lam[:, 1:2], lam[:, 0:1], ACT.Exp, scale=-1.0).then_inc(s["act_const"], 1)
            act.wait_ge(s["pe_const"], 5)
            a.activation(small[:, 0:E], ps_g[:, 0:E], ACT.Sqrt).then_inc(s["act_const"], 1)

            def turn(i, last):
                for pr in range(2):
                    pair = i * 2 + pr
                    act.wait_ge(s["stats"], pair + 1)
                    a.activation(rstd[pr], ve[pr], ACT.Sqrt).then_inc(s["std"], 1)
                    for w in range(2):
                        n = 2 * pr + w
                        uu = i * 4 + n
                        act.wait_ge(w_in[n], i * 16 + 16)
                        a.activation(whi[:, bass.ds(uu * UW, UW)], raw[n], ACT.Abs,
                                     accum_out=wsum[:, n:n + 1]).then_inc(s["wsum_ok"], 1)
                    for h in range(2):
                        for k in range(K):
                            m = (2 * pr + h) * K + k
                            act.wait_ge(s["xt_ok"], i * (4 * K) + (m + 1))
                            if not (isinstance(i, int) and i == 0 and pr == 0):
                                act.wait_ge(s["bu_ok"], pair)
                            a.copy(xnt[h][:, k, :], ps_t[:, k * S:(k + 1) * S]).then_inc(s["xt_out"], 1)
                    for w in range(2):
                        n = 2 * pr + w
                        uu = i * 4 + n
                        act.wait_ge(s["wscale_ok"], uu + 1)
                        a.activation(whi[:, bass.ds(uu * UW, UW)], raw[n], ACT.Copy,
                                     scale=scale_w[:, bass.ds(uu, 1)]).then_inc(s["whi_ok"], 1)
                    if not last:
                        for w in range(2):
                            n = 2 * pr + w
                            e2 = act.snap(i * 2 + (pr + 2), min_val=0, max_val=E - 1) if not isinstance(i, int) else i * 2 + pr + 2
                            act.wait_ge(s["wlo_ok"], i * 4 + (n + 1))
                            wload(e2, w, n)
            turn(0, False)
            with act.Fori(1, PAIRS // 2 - 1) as i:
                turn(i, False)
            turn(PAIRS // 2 - 1, True)

            act.wait_ge(s["r_dve"], 1)
            a.activation(sq0, xnorm, ACT.Sqrt).then_inc(s["r_act"], 1)
            act.wait_ge(s["wlo_ok"], 2 * E)
            a.activation(gelu_b, b1t[:, :], ACT.Gelu).then_inc(s["r_act"], 1)
            act.wait_ge(s["r_dve"], 4)
            a.activation(small[:, 20:21], small[:, 19:20], ACT.Exp, scale=-1.0).then_inc(s["r_act"], 1)

            def split_x(j, p):
                act.wait_ge(s["f_xt"], j + 1)
                if not (isinstance(j, int) and j < 2):
                    act.wait_ge(s["f_h"], (j - 1) * 2)
                a.activation(xhi[p].rearrange("p k t -> p (k t)"), ps_x[p][:, 0:D], ACT.Copy,
                             scale=XS).then_inc(s["f_xhi"], 1)

            def hidden(j, p):
                e = act.value_load(tile_expert[0:1, bass.ds(j, 1)], min_val=0, max_val=E - 1)
                for half in range(2):
                    act.wait_ge(s["f_h"], j * 2 + (1 + half))
                    if half == 0 and not (isinstance(j, int) and j < 2):
                        act.wait_ge(s["f_hlo"], (j - 1) * 2)
                    for c in range(half * C // 2, (half + 1) * C // 2):
                        ins = a.activation(h32[p][:, c * P:(c + 1) * P], ps_h[p][:, c * P:(c + 1) * P], ACT.Gelu,
                                           bias=b1t[:, bass.ds(e * C + c, 1)], scale=inv_in[:, bass.ds(e, 1)])
                    ins.then_inc(s["f_gelu"], 1)
            act.wait_ge(s["idx_ok"], 1)
            split_x(0, 0)
            split_x(1, 1)
            hidden(0, 0)

            def step(i):
                for p in range(2):
                    split_x(i * 2 + p, p)
                    hidden(i * 2 + (p - 1), 1 - p)
            step(1)
            with act.Fori(2, NT // 2) as i:
                step(i)
            hidden(NT - 1, 1)

        @block.tensor
        def _(pe):
            t = nc.tensor
            pe.wait_ge(s["params_in"], PARAMS)
            pe.wait_ge(s["consts"], 1)
            for k in range(K):
                t.transpose(ps_s[:, k * N:(k + 1) * N], st_b[:, k * P:(k + 1) * P], ident[0:N, 0:N])
            last = t.transpose(ps_s[:, 128 + 0:128 + P], st_c[:, 0, :, :].rearrange("p r n -> p (r n)"), ident[:])
            last = t.transpose(ps_s[:, 128 + P:128 + 2 * P], st_c[:, 1, :, :].rearrange("p r n -> p (r n)"), ident[:])
            last.then_inc(s["pe_const"], 1)
            for k in range(K):
                last = t.transpose(ps_s[:, 384 + k * E:384 + (k + 1) * E], st_w[:, k * P:(k + 1) * P], ident[0:E, 0:E])
            last.then_inc(s["pe_const"], 1)
            t.transpose(ps_g[:, 64:64 + E * C], st_b1, ident[0:E * C, 0:E * C]).then_inc(s["pe_const"], 1)
            t.matmul(ps_g[:, 128:128 + D], ones[0:E, :], st_b2, start=True, stop=True).then_inc(s["pe_const"], 1)
            pe.wait_ge(s["dve_const"], 1)
            for k in range(K):
                last = t.matmul(ps_g[:, 0:E], ones[:], watsq[:, k * E:(k + 1) * E], start=(k == 0), stop=(k == K - 1))
            last.then_inc(s["pe_const"], 1)

            def turn(i):
                for pr in range(2):
                    pair = i * 2 + pr
                    for h in range(2):
                        bat = i * 4 + (2 * pr + h)
                        pe.wait_ge(s["xn_ok"], bat + 1)
                        for k in range(K):
                            if not (isinstance(i, int) and i == 0 and pr == 0 and h == 0):
                                pe.wait_ge(s["xt_out"], bat * K + (k + 1 - K))
                            for q in range(Q):
                                last = t.transpose(ps_t[:, k * S + q * P:k * S + (q + 1) * P],
                                                   xnb[h][:, q, k * P:(k + 1) * P], ident[:])
                            last.then_inc(s["xt_ok"], 1)
                    for h in range(2):
                        bat = i * 4 + (2 * pr + h)
                        pe.wait_ge(s["xt_out"], bat * K + K)
                        for q in range(Q):
                            for k in range(K):
                                last = t.matmul(ps_num[:, bass.ds(bat * E + q * B * E, E)],
                                                xnt[h][:, k, q * P:(q + 1) * P], wat[:, k * E:(k + 1) * E],
                                                start=(k == 0), stop=(k == K - 1))
                        last.then_inc(s["num_ok"], 1)
                        if h == 0 and not (isinstance(i, int) and i == 0 and pr == 0):
                            pe.wait_ge(s["scan_ok"], pair)
                        for k in range(K):
                            last = t.matmul(ps_bu[h * N:(h + 1) * N, :], bt[:, k * N:(k + 1) * N], xnt[h][:, k, :],
                                            start=(k == 0), stop=(k == K - 1))
                    last.then_inc(s["bu_ok"], 1)
                    pe.wait_ge(s["scan_ok"], pair + 1)
                    for h in range(2):
                        bat = i * 4 + (2 * pr + h)
                        if not (isinstance(i, int) and i == 0 and pr == 0 and h == 0):
                            pe.wait_ge(s["base_ok"], bat)
                        for q in range(Q):
                            last = t.matmul(ps_y[:, q * D:(q + 1) * D], hs[pr][h * N:(h + 1) * N, q * P:(q + 1) * P],
                                            ct[h * N:(h + 1) * N, :], start=True, stop=True)
                        last.then_inc(s["y_ok"], 1)
            pe.wait_ge(s["dve_const"], 2)
            turn(0)
            with pe.Fori(1, PAIRS // 2) as i:
                turn(i)

            pe.wait_ge(s["oh_pos"], 1)
            pe.wait_ge(s["r_pool2"], 1)
            t.matmul(ps_s[:, 0:TE], tri16, oh16, start=True, stop=True)
            t.matmul(ps_bu[:, 0:TE], ones16, oh16, start=True, stop=True).then_inc(s["r_pe"], 1)
            pe.wait_ge(s["g_dve"], 1)
            for e in range(E):
                if e >= 2:
                    pe.wait_ge(s["g_dve"], e)
                dst = (ps_g, ps_num)[e % 2][:, 0:D]
                for c in range(C):
                    n = e * C + c
                    w2h = whi[:, (2 * e + 1) * UW + c * D:(2 * e + 1) * UW + (c + 1) * D]
                    w2l = wlo[:, (2 * e + 1) * UW + c * D:(2 * e + 1) * UW + (c + 1) * D]
                    gh = gb16[:, n:n + 1].to_broadcast([P, P])
                    gl = gb16[:, E * C + n:E * C + n + 1].to_broadcast([P, P])
                    t.matmul(dst, gh, w2h, start=(c == 0), stop=False)
                    t.matmul(dst, gh, w2l, start=False, stop=False)
                    last = t.matmul(dst, gl, w2h, start=False, stop=(c == C - 1))
                last.then_inc(s["g_pe"], 1)
            pe.wait_ge(s["r_dve"], 3)
            for q in range(Q):
                last = t.transpose(ps_t[:, q * P:(q + 1) * P], aff[:, q * P:(q + 1) * P], ident[:])
            last.then_inc(s["r_pe"], 1)
            t.matmul(ps_y[:, 0:1], ones[:], small[:, 16:17], start=True, stop=True).then_inc(s["r_pe"], 1)
            pe.wait_ge(s["oh_pos"], 2)
            for tt in range(T):
                last = t.matmul(ps_s[:, 0:2 * NT], lo16[:, tt, :], v16[:, :, tt, :], start=(tt == 0), stop=(tt == T - 1))
            last.then_inc(s["inv_pe"], 1)
            pe.wait_ge(s["oh_pos"], 3)
            for q in range(Q):
                last = t.transpose(ps_t[:, S + q * P:S + (q + 1) * P], eq_rows[:, q * P:(q + 1) * P], ident[:])
            last.then_inc(s["r_pe"], 1)
            pe.wait_ge(s["oh_pos"], 4)
            for tt in range(T):
                last = t.matmul(ps_s[:, 256:256 + NT], lo16[:, tt, :], v16[:, 0, tt, :], start=(tt == 0), stop=(tt == T - 1))
            last.then_inc(s["inv_pe"], 1)

            gx = [s["gx0"], s["gx1"]]

            def rows_t(j, p, k):
                pe.wait_ge(gx[p], k * 16 + 16)
                if not (isinstance(j, int) and j < 2):
                    pe.wait_ge(s["f_xlo"], j - 1)
                for kk in range(K):
                    last = t.transpose(ps_x[p][:, kk * P:(kk + 1) * P], xg[p][:, kk * P:(kk + 1) * P], ident[:])
                last.then_inc(s["f_xt"], 1)

            def up(j, p):
                e = pe.value_load(tile_expert[0:1, bass.ds(j, 1)], min_val=0, max_val=E - 1)
                w0 = pe.snap(e * (2 * UW))
                pe.wait_ge(s["f_xlo"], j + 1)
                if not (isinstance(j, int) and j < 2):
                    pe.wait_ge(s["f_gelu"], (j - 1) * 2)
                for c in range(C):
                    dst = ps_h[p][:, c * P:(c + 1) * P]
                    for k in range(K):
                        wh = whi[:, bass.ds(w0 + (k * F + c * P), P)]
                        wl = wlo[:, bass.ds(w0 + (k * F + c * P), P)]
                        t.matmul(dst, wh, xhi[p][:, k, :], start=(k == 0), stop=False)
                        t.matmul(dst, wh, xlo[p][:, k, :], start=False, stop=False)
                        last = t.matmul(dst, wl, xhi[p][:, k, :], start=False, stop=(k == K - 1))
                    if c % (C // 2) == C // 2 - 1:
                        last.then_inc(s["f_h"], 1)

            def down(j, p):
                e = pe.value_load(tile_expert[0:1, bass.ds(j, 1)], min_val=0, max_val=E - 1)
                w0 = pe.snap(e * (2 * UW) + UW)
                if not (isinstance(j, int) and j < 2):
                    pe.wait_ge(s["f_yr"], j - 1)
                for c in range(C):
                    if c % (C // 2) == 0:
                        pe.wait_ge(s["f_hlo"], j * 2 + (1 + c // (C // 2)))
                    dst = ps_o[p][:, 0:D]
                    wh = whi[:, bass.ds(w0 + c * D, D)]
                    wl = wlo[:, bass.ds(w0 + c * D, D)]
                    hh = hhi[p][:, c * P:(c + 1) * P]
                    hl = hlo[p][:, c * P:(c + 1) * P]
                    t.matmul(dst, hh, wh, start=(c == 0), stop=False)
                    t.matmul(dst, hh, wl, start=False, stop=False)
                    last = t.matmul(dst, hl, wh, start=False, stop=(c == C - 1))
                last.then_inc(s["f_y"], 1)
            pe.wait_ge(s["idx_ok"], 1)
            rows_t(0, 0, 0)
            rows_t(1, 1, 0)
            up(0, 0)

            def step(i):
                rows_t(i * 2, 0, i)
                up(i * 2 - 1, 1)
                down(i * 2 - 2, 0)
                rows_t(i * 2 + 1, 1, i)
                up(i * 2, 0)
                down(i * 2 - 1, 1)
            step(1)
            with pe.Fori(2, NT // 2) as i:
                step(i)
            up(NT - 1, 1)
            down(NT - 2, 0)
            down(NT - 1, 1)

        @block.vector
        def _(dve):
            v = nc.vector
            link_n = [0]

            def link(ins):
                link_n[0] += 1
                ins.then_inc(s["dve_chain"], 1)
                dve.wait_ge(s["dve_chain"], link_n[0])

            def power_of_two(dst, src, n, exps):
                link(v.tensor_scalar(exps, src.bitcast(I32), 23, None, ALU.logical_shift_right))
                link(v.tensor_scalar(exps, exps, -1.0, 268.0, ALU.mult, ALU.add))
                link(v.tensor_scalar(exps, exps, 250.0, 4.0, ALU.min, ALU.max))
                link(v.tensor_scalar(dst.bitcast(I32), exps, 23, None, ALU.logical_shift_left))

            dve.wait_ge(s["pe_const"], 2)
            v.tensor_copy(bt[:, :], ps_s[:, 0:K * N])
            v.tensor_copy(ct[:, :], ps_s[:, 128:128 + D])
            link(v.tensor_copy(wat[:, :], ps_s[:, 384:384 + K * E]))
            v.tensor_tensor(watsq, wat[:, :], wat[:, :], ALU.mult).then_inc(s["dve_const"], 1)
            dve.wait_ge(s["pe_const"], 5)
            dve.wait_ge(s["act_const"], 1)
            link(v.tensor_scalar(lam[:, 2:3], lam[:, 1:2], 1.0, None, ALU.add))
            link(v.reciprocal(lam[:, 3:4], lam[:, 2:3]))
            dve.wait_ge(s["act_const"], 2)
            v.tensor_copy(b1t[:, :], ps_g[:, 64:64 + E * C])
            v.tensor_copy(c_bc[:, :], ps_g[:, 128:128 + D])
            link(v.tensor_scalar(small[:, 8:16], small[:, 0:8], 1e-30, None, ALU.max))
            link(v.reciprocal(small[:, 24:32], small[:, 8:16]))
            link(v.tensor_tensor(small[:, 32:40], small[:, 24:32], ps_g[:, 0:E], ALU.mult))
            link(v.tensor_tensor(small[:, 8:16], small[:, 0:8], small[:, 32:40], ALU.add))
            link(v.tensor_scalar(wnorm[:, :], small[:, 8:16], 0.5, None, ALU.mult))
            v.memset(cnt[:, 0:1], 0.0).then_inc(s["dve_const"], 1)

            def stats_of(pair, nb, first):
                pr = nb // 2
                for h in range(2):
                    n = nb + h
                    if isinstance(pair, int):
                        dve.wait_ge(x_in[n], 16 * (pair // 2 + 1))
                    else:
                        dve.wait_ge(x_in[n], first)
                    for q in range(Q):
                        c = (h * Q + q) * 6
                        last = v.bn_stats(stats[:, c:c + 6], xb[n][:, q, :])
                last.then_inc(s["r_dve2"], 1)
                dve.wait_ge(s["r_dve2"], pair * 2 + 1)
                v.memset(cnt[:, 4:5], 0.0)
                for c in range(2 * Q):
                    last = v.bn_aggr(mv[pr][:, 2 * c:2 * c + 2], stats[:, c * 6:(c + 1) * 6])
                last.then_inc(s["r_dve2"], 1)
                dve.wait_ge(s["r_dve2"], pair * 2 + 2)
                v.tensor_scalar(ve[pr], mv[pr].rearrange("p (t m) -> p t m", m=2)[:, :, 1],
                                EPS, None, ALU.add).then_inc(s["stats"], 1)

            def rstd_of(pair, pr):
                r_ = rstd[pr]
                v_ = ve[pr]
                nw = s["newton"]
                dve.wait_ge(s["std"], pair + 1)
                v.reciprocal(r_, r_).then_inc(nw, 1)
                dve.wait_ge(nw, pair * 5 + 1)
                v.tensor_tensor(newt[:, :], r_, r_, ALU.mult).then_inc(nw, 1)
                dve.wait_ge(nw, pair * 5 + 2)
                v.tensor_tensor(newt[:, :], newt[:, :], v_, ALU.mult).then_inc(nw, 1)
                dve.wait_ge(nw, pair * 5 + 3)
                v.tensor_scalar(newt[:, :], newt[:, :], -0.5, 1.5, ALU.mult, ALU.add).then_inc(nw, 1)
                dve.wait_ge(nw, pair * 5 + 4)
                v.tensor_tensor(r_, r_, newt[:, :], ALU.mult).then_inc(nw, 1)
                dve.wait_ge(nw, pair * 5 + 5)
                v.tensor_tensor(newt[:, :], mv[pr].rearrange("p (t m) -> p t m", m=2)[:, :, 1], r_,
                                ALU.mult).then_inc(s["ratio_c"], 1)
                dve.wait_ge(s["ratio_c"], pair + 1)
                v.tensor_tensor(ratio_all[:, bass.ds(pair * (2 * Q), 2 * Q)], newt[:, :], r_, ALU.mult)

            def turn(i, last_turn):
                for pr in range(2):
                    pair = i * 2 + pr
                    for h in range(2):
                        n = 2 * pr + h
                        bat = i * 4 + n
                        if not (isinstance(i, int) and i == 0 and pr == 0):
                            dve.wait_ge(s["xt_ok"], (bat - 1) * K)
                            dve.wait_ge(s["dx_ok"], (bat - 2) * 2 + 1)
                            dve.wait_ge(xn_out[h], pair * 16)
                        for q in range(Q):
                            tt = h * Q + q
                            last = v.tensor_scalar(xnb[h][:, q, :], xb[n][:, q, :], mv[pr][:, 2 * tt:2 * tt + 1],
                                                   rstd[pr][:, tt:tt + 1], ALU.subtract, ALU.mult)
                        last.then_inc(s["xn_ok"], 1)
                    final = last_turn and pr == 1
                    if not final:
                        stats_of(pair + 1, 2 * (1 - pr), i * 16 + 16 * (1 + pr))
                    for w in range(2):
                        uu = i * 4 + (2 * pr + w)
                        ws = s["wchain"]
                        dve.wait_ge(s["wmax_ok"], uu + 1)
                        ex = exp_w[:, bass.ds(uu, 1)]
                        v.tensor_scalar(ex, wmax[:, 2 * pr + w:2 * pr + w + 1].bitcast(I32), 23, None,
                                        ALU.logical_shift_right).then_inc(ws, 1)
                        dve.wait_ge(ws, uu * 3 + 1)
                        v.tensor_scalar(ex, ex, -1.0, 268.0, ALU.mult, ALU.add).then_inc(ws, 1)
                        dve.wait_ge(ws, uu * 3 + 2)
                        v.tensor_scalar(ex, ex, 250.0, 4.0, ALU.min, ALU.max).then_inc(ws, 1)
                        dve.wait_ge(ws, uu * 3 + 3)
                        v.tensor_scalar(scale_w[:, bass.ds(uu, 1)].bitcast(I32), ex, 23, None,
                                        ALU.logical_shift_left).then_inc(s["wscale_ok"], 1)
                    for w in range(2):
                        n = 2 * pr + w
                        uu = i * 4 + n
                        dve.wait_ge(s["whi_ok"], uu + 1)
                        v.scalar_tensor_tensor(out=wlo[:, bass.ds(uu * UW, UW)], in0=raw[n],
                                               scalar=scale_w[:, bass.ds(uu, 1)], in1=whi[:, bass.ds(uu * UW, UW)],
                                               op0=ALU.mult, op1=ALU.subtract).then_inc(s["wlo_ok"], 1)
                    if not final:
                        rstd_of(pair + 1, 1 - pr)
                    dve.wait_ge(s["bu_ok"], pair + 1)
                    v.tensor_tensor_scan(hs[pr], lam_c.to_broadcast([P, S]), ps_bu[:, :], 0.0, ALU.mult,
                                         ALU.add).then_inc(s["scan_ok"], 1)
                    for h in range(2):
                        n = 2 * pr + h
                        bat = i * 4 + n
                        dve.wait_ge(s["y_ok"], bat + 1)
                        dve.wait_ge(s["dx_ok"], bat * 2 + 2)
                        xf = xb[n].rearrange("p q d -> p (q d)")
                        v.tensor_tensor(xf, ps_y[:, :], xf, ALU.add).then_inc(s["base_ok"], 1)
            stats_of(0, 0, None)
            rstd_of(0, 0)
            turn(0, False)
            with dve.Fori(1, PAIRS // 2 - 1) as i:
                turn(i, False)
            turn(PAIRS // 2 - 1, True)

            for n in range(4):
                dve.wait_ge(base_out[n], 16 * (B // 4))
            for n in range(2):
                dve.wait_ge(xn_out[n], 16 * (B // 2))
            dve.wait_ge(s["num_ok"], B)
            def te(x):
                return x.rearrange("p (t e) -> p t e", e=E)
            def bt_(x):
                return x.rearrange("p (t a) -> p t a", a=1).to_broadcast([P, T, E])
            def be_(x):
                return x.rearrange("p (a e) -> p a e", a=1).to_broadcast([P, T, E])
            link(v.tensor_copy(xnorm.rearrange("p (q b) -> p q b", q=Q), ratio_all[:, :].rearrange("p (b q) -> p q b", q=Q)))
            v.tensor_scalar(cnt[:, 1:2], cnt[:, 0:1], 1.0, None, ALU.add).then_inc(s["r_dve"], 1)
            dve.wait_ge(s["r_act"], 1)
            link(v.tensor_scalar(sq1, sq0, 1e-30, None, ALU.max))
            link(v.reciprocal(ratio, sq1))
            link(v.tensor_tensor(sq1, ratio, xnorm, ALU.mult))
            link(v.tensor_tensor(ratio, sq1, sq0, ALU.add))
            link(v.tensor_scalar(xnorm, ratio, 0.5 * float(D) ** 0.5, None, ALU.mult))
            link(v.tensor_tensor(te(den), bt_(xnorm), be_(wnorm[:, :]), ALU.mult))
            link(v.tensor_scalar(den, den, 1e-9, None, ALU.add))
            link(v.reciprocal(diff, den))
            link(v.tensor_tensor(aff, ps_num[:, 0:TE], diff, ALU.mult))
            link(v.tensor_reduce(rowmax, te(aff), AX.X, ALU.max))
            link(v.tensor_tensor(te(diff), te(aff), bt_(rowmax), ALU.subtract))
            link(v.tensor_scalar(small[:, 40:48], iota_f[:, 0:E], -1.0, float(E), ALU.mult, ALU.add))
            link(v.scalar_tensor_tensor(out=te(den), in0=te(diff), scalar=NEAR, in1=be_(small[:, 40:48]),
                                        op0=ALU.is_ge, op1=ALU.mult))
            link(v.tensor_reduce(best, te(den), AX.X, ALU.max))
            v.tensor_tensor(te(oh16), be_(small[:, 40:48]), bt_(best), ALU.is_equal).then_inc(s["oh_pos"], 1)

            link(v.tensor_reduce(small[:, 48:56], b1t[:, :].rearrange("p (e c) -> p e c", c=C), AX.X, ALU.max,
                                 apply_absolute_value=True))
            v.tensor_scalar(cnt[:, 1:2], cnt[:, 0:1], 1.0, None, ALU.add).then_inc(s["r_dve"], 1)
            dve.wait_ge(s["r_pool2"], 2)
            ew = exp_w[:, :].rearrange("p (e w) -> p e w", w=2)
            link(v.tensor_scalar(tmp_i[:, 0:E], ew[:, :, 0], -1.0, 254.0 - 11.0, ALU.mult, ALU.add))
            link(v.tensor_scalar(tmp_i[:, 0:E], tmp_i[:, 0:E], 1.0, None, ALU.max))
            link(v.tensor_scalar(inv_in[:, :].bitcast(I32), tmp_i[:, 0:E], 23, None, ALU.logical_shift_left))
            link(v.scalar_tensor_tensor(out=small[:, 48:56],
                                        in0=inv_in[:, :], scalar=float(D) * 2.0 ** 15 * XS,
                                        in1=small[:, 56:64], op0=ALU.mult, op1=ALU.add))
            power_of_two(h_scale[:, :], small[:, 48:56], E, exp_h[:, :])
            link(v.tensor_tensor(tmp_i[:, 0:E], ew[:, :, 1], exp_h[:, :], ALU.add) if False else
                 v.scalar_tensor_tensor(out=tmp_i[:, 0:E], in0=ew[:, :, 1], scalar=-1.0, in1=exp_h[:, :],
                                        op0=ALU.mult, op1=ALU.subtract))
            link(v.tensor_scalar(tmp_i[:, 0:E], tmp_i[:, 0:E], 381.0, None, ALU.add))
            link(v.tensor_scalar(tmp_i[:, 0:E], tmp_i[:, 0:E], 1.0, 254.0, ALU.max, ALU.min))
            link(v.tensor_scalar(inv_out[:, :].bitcast(I32), tmp_i[:, 0:E], 23, None, ALU.logical_shift_left))
            dve.wait_ge(s["r_act"], 2)
            gv = gelu_b.rearrange("p (e c) -> p e c", c=C)
            hb = h_scale[:, :].rearrange("p (e a) -> p e a", a=1).to_broadcast([P, E, C])
            link(v.tensor_tensor(gv, gv, hb, ALU.mult))
            link(v.tensor_copy(gb16[:, 0:E * C], gelu_b))
            v.tensor_tensor(gb16[:, E * C:2 * E * C], gelu_b, gb16[:, 0:E * C], ALU.subtract).then_inc(s["g_dve"], 1)

            dve.wait_ge(s["r_pe"], 1)
            link(v.tensor_copy(cnt_e.rearrange("p (e t) -> p t e", e=E), te(ps_bu[:, 0:TE])))
            ce = cnt_e.rearrange("p (e t) -> p e t", e=E)
            link(v.tensor_tensor_scan(scan_e, ones[:, 0:1].to_broadcast([P, TE]), cnt_e, 0.0, ALU.mult, ALU.add))
            link(v.tensor_tensor(scan_e, scan_e, cnt_e, ALU.subtract))
            n_e, tiles_e, t_incl, adj = small[:, 0:8], small[:, 8:16], small[:, 24:32], small[:, 32:40]
            link(v.tensor_reduce(n_e, ce, AX.X, ALU.add))
            link(v.tensor_scalar(sq0, iota_f[:, 0:T], float(P), None, ALU.mult))
            link(v.tensor_tensor(diff.rearrange("p (e t) -> p e t", e=E),
                                 n_e.rearrange("p (e a) -> p e a", a=1).to_broadcast([P, E, T]),
                                 sq0.rearrange("p (a t) -> p a t", a=1).to_broadcast([P, E, T]), ALU.is_gt))
            link(v.tensor_reduce(tiles_e, diff.rearrange("p (e t) -> p e t", e=E), AX.X, ALU.add))
            link(v.tensor_tensor_scan(t_incl, ones[:, 0:E], tiles_e, 0.0, ALU.mult, ALU.add))
            link(v.tensor_tensor(adj, t_incl, tiles_e, ALU.subtract))
            link(v.tensor_tensor_scan(tiles_e, ones[:, 0:E], n_e, 0.0, ALU.mult, ALU.add))
            link(v.tensor_tensor(tiles_e, tiles_e, n_e, ALU.subtract))
            link(v.scalar_tensor_tensor(out=adj, in0=adj, scalar=float(P), in1=tiles_e, op0=ALU.mult, op1=ALU.subtract))
            link(v.tensor_tensor(scan_e.rearrange("p (e t) -> p e t", e=E), scan_e.rearrange("p (e t) -> p e t", e=E),
                                 adj.rearrange("p (e a) -> p e a", a=1).to_broadcast([P, E, T]), ALU.add))
            link(v.tensor_tensor(te(pos4), te(ps_s[:, 0:TE]), scan_e.rearrange("p (e t) -> p t e", e=E), ALU.add))
            link(v.tensor_tensor(pos4, pos4, oh16, ALU.mult))
            link(v.tensor_reduce(pos, te(pos4), AX.X, ALU.add))
            link(v.tensor_copy(pos_i, pos))
            link(v.tensor_scalar(hi_i, pos_i, 7, None, ALU.logical_shift_right))
            link(v.tensor_scalar(lo_i, pos_i, P - 1, None, ALU.bitwise_and))
            link(v.tensor_copy(hi_f, hi_i))
            link(v.tensor_copy(lo_f, lo_i))
            tc = tcmp.rearrange("p (j e) -> p j e", e=E)
            link(v.tensor_tensor(tc, iota_f[:, 0:NT].rearrange("p (j a) -> p j a", a=1).to_broadcast([P, NT, E]),
                                 t_incl.rearrange("p (a e) -> p a e", a=1).to_broadcast([P, NT, E]), ALU.is_ge))
            link(v.tensor_reduce(mask_slot, tc, AX.X, ALU.add))
            link(v.tensor_scalar(mask_slot, mask_slot, float(E - 1), None, ALU.min))
            link(v.tensor_copy(tile_expert, mask_slot))

            link(v.tensor_reduce(small[:, 16:17], aff, AX.X, ALU.add))
            v.tensor_scalar(cnt[:, 1:2], cnt[:, 0:1], 1.0, None, ALU.add).then_inc(s["r_dve"], 1)

            v.tensor_tensor(lo16, iota_f[:, :].rearrange("p (a l) -> p a l", a=1).to_broadcast([P, T, P]),
                            lo_f.rearrange("p (t a) -> p t a", a=1).to_broadcast([P, T, P]), ALU.is_equal)
            link(v.tensor_tensor(e16, iota_f[:, 0:NT].rearrange("p (a j) -> p a j", a=1).to_broadcast([P, T, NT]),
                                 hi_f.rearrange("p (t a) -> p t a", a=1).to_broadcast([P, T, NT]), ALU.is_equal))
            v.tensor_scalar(v16[:, 0], e16, pcol[:, 0:1], None, ALU.mult)
            v.tensor_tensor(v16[:, 1], e16, tnum.rearrange("p (t a) -> p t a", a=1).to_broadcast([P, T, NT]),
                            ALU.mult).then_inc(s["oh_pos"], 1)
            for e in range(E):
                dve.wait_ge(s["g_pe"], e + 1)
                v.tensor_scalar(g_bc[:, e * D:(e + 1) * D], (ps_g, ps_num)[e % 2][:, 0:D],
                                inv_out[:, e:e + 1], None, ALU.mult).then_inc(s["g_dve"], 1)
                dve.wait_ge(s["g_dve"], e + 2)
                link(v.tensor_tensor(c_bc[:, :], c_bc[:, :], g_bc[:, e * D:(e + 1) * D], ALU.add))
            dve.wait_ge(s["inv_pe"], 1)
            iv = mask_slot
            link(v.tensor_scalar(iv, ps_s[:, 0:NT], 0.5, float(4 * TOKENS), ALU.is_lt, ALU.mult))
            link(v.tensor_tensor(iv, ps_s[:, 0:NT], iv, ALU.add))
            link(v.scalar_tensor_tensor(out=iv, in0=ps_s[:, NT:2 * NT], scalar=float(P), in1=iv, op0=ALU.mult, op1=ALU.add))
            link(v.tensor_scalar(iv, iv, -1.0, None, ALU.add))
            link(v.tensor_copy(idx_all, iv))

            dve.wait_ge(s["r_pe"], 3)
            z, cap = small[:, 19:20], small[:, 21:22]
            link(v.tensor_scalar(small[:, 18:19], ps_y[:, 0:1], 1.0 / (TOKENS * E), None, ALU.mult))
            link(v.tensor_tensor(z, small[:, 18:19], thr_bc[:, :], ALU.subtract))
            v.tensor_scalar(cnt[:, 1:2], cnt[:, 0:1], 1.0, None, ALU.add).then_inc(s["r_dve"], 1)
            dve.wait_ge(s["r_act"], 3)
            link(v.tensor_scalar(small[:, 17:18], small[:, 20:21], 1.0, None, ALU.add))
            link(v.reciprocal(small[:, 18:19], small[:, 17:18]))
            link(v.tensor_scalar(cap, small[:, 18:19], float(S), None, ALU.mult))
            link(v.tensor_copy(tmp_i[:, 0:1], cap))
            link(v.tensor_copy(small[:, 17:18], tmp_i[:, 0:1]))
            link(v.tensor_tensor(small[:, 18:19], small[:, 17:18], cap, ALU.is_gt))
            link(v.tensor_tensor(cap, small[:, 17:18], small[:, 18:19], ALU.subtract))
            link(v.tensor_scalar(cap, cap, 4.0, float(S), ALU.max, ALU.min))

            link(v.tensor_copy(a_rows, ps_t[:, 0:S]))
            sign, kth, kneg = small[:, 22:23], small[:, 23:24], small[:, 24:25]
            link(v.tensor_scalar(eq_rows, a_rows, 0.0, 0.0, ALU.is_ge, ALU.add, accum_out=cnt[:, 2:3]))
            link(v.tensor_tensor(kneg, cnt[:, 2:3], cap, ALU.is_lt))
            link(v.tensor_scalar(sign, kneg, -2.0, 1.0, ALU.mult, ALU.add))
            link(v.tensor_scalar(small[:, 25:26], cap, -2.0, float(S + 1), ALU.mult, ALU.add))
            link(v.scalar_tensor_tensor(out=kth, in0=small[:, 25:26], scalar=kneg, in1=cap, op0=ALU.mult, op1=ALU.add))
            srch = aff
            link(v.tensor_scalar(srch, a_rows, sign, None, ALU.mult))
            cand, tb = bits[:, 0:1], bits[:, 1:2]
            link(v.memset(cand, 1 << 30))
            for bit in range(30, -1, -1):
                link(v.tensor_scalar(eq_rows, srch, cand.bitcast(F32), 0.0, ALU.is_ge, ALU.add, accum_out=cnt[:, 2:3]))
                link(v.tensor_scalar(tb, cnt[:, 2:3], kth, float(1 << bit), ALU.is_lt, ALU.mult))
                if bit:
                    link(v.scalar_tensor_tensor(out=cand, in0=tb, scalar=1 << (bit - 1), in1=cand,
                                                op0=ALU.bitwise_or, op1=ALU.bitwise_xor))
                else:
                    link(v.tensor_tensor(cand, tb, cand, ALU.bitwise_xor))
            thr = small[:, 26:27]
            link(v.tensor_tensor(thr, cand.bitcast(F32), sign, ALU.mult))
            gt = aff
            link(v.tensor_scalar(gt, a_rows, thr, 0.0, ALU.is_gt, ALU.add, accum_out=cnt[:, 3:4]))
            link(v.tensor_tensor(small[:, 27:28], cap, cnt[:, 3:4], ALU.subtract))
            link(v.tensor_scalar(eq_rows, a_rows, thr, None, ALU.is_equal))
            link(v.tensor_tensor_scan(a_rows, ones[:, 0:1].to_broadcast([P, S]), eq_rows, 0.0, ALU.mult, ALU.add))
            link(v.scalar_tensor_tensor(out=eq_rows, in0=a_rows, scalar=small[:, 27:28], in1=eq_rows,
                                        op0=ALU.is_le, op1=ALU.mult))
            v.tensor_tensor(eq_rows, eq_rows, gt, ALU.add).then_inc(s["oh_pos"], 1)
            dve.wait_ge(s["r_pe"], 4)
            link(v.tensor_tensor(aff, ps_t[:, S:2 * S], oh16, ALU.mult))
            link(v.tensor_reduce(mtok, te(aff), AX.X, ALU.add))
            v.tensor_tensor(v16[:, 0], e16, mtok.rearrange("p (t a) -> p t a", a=1).to_broadcast([P, T, NT]),
                            ALU.mult).then_inc(s["oh_pos"], 1)
            dve.wait_ge(s["inv_pe"], 2)
            v.tensor_copy(mask_slot, ps_s[:, 256:256 + NT]).then_inc(s["idx_ok"], 1)

            gb = [s["gb0"], s["gb1"]]
            sc = [s["sc0"], s["sc1"]]

            def x_low(j, p):
                dve.wait_ge(s["f_xhi"], j + 1)
                v.scalar_tensor_tensor(out=xlo[p].rearrange("p k t -> p (k t)"), in0=ps_x[p][:, 0:D], scalar=XS,
                                       in1=xhi[p].rearrange("p k t -> p (k t)"), op0=ALU.mult,
                                       op1=ALU.subtract).then_inc(s["f_xlo"], 1)

            def h_parts(j, p):
                e = dve.value_load(tile_expert[0:1, bass.ds(j, 1)], min_val=0, max_val=E - 1)
                for half in range(2):
                    cs = slice(half * F // 2, (half + 1) * F // 2)
                    dve.wait_ge(s["f_gelu"], j * 2 + (1 + half))
                    if half == 0 and not (isinstance(j, int) and j < 2):
                        dve.wait_ge(s["f_y"], j - 1)
                    v.tensor_scalar(hhi[p][:, cs], h32[p][:, cs], h_scale[:, bass.ds(e, 1)], None,
                                    ALU.mult).then_inc(s["f_hhi"], 1)
                    dve.wait_ge(s["f_hhi"], j * 2 + (1 + half))
                    v.scalar_tensor_tensor(out=hlo[p][:, cs], in0=h32[p][:, cs], scalar=h_scale[:, bass.ds(e, 1)],
                                           in1=hhi[p][:, cs], op0=ALU.mult, op1=ALU.subtract).then_inc(s["f_hlo"], 1)

            def result(j, p, k):
                e = dve.value_load(tile_expert[0:1, bass.ds(j, 1)], min_val=0, max_val=E - 1)
                dve.wait_ge(s["f_y"], j + 1)
                v.scalar_tensor_tensor(out=yr[p], in0=ps_o[p][:, 0:D], scalar=inv_out[:, bass.ds(e, 1)],
                                       in1=g_bc[:, bass.ds(e * D, D)], op0=ALU.mult,
                                       op1=ALU.subtract).then_inc(s["f_yr"], 1)
                dve.wait_ge(s["f_yr"], j + 1)
                dve.wait_ge(gb[p], k * 16 + 16)
                v.scalar_tensor_tensor(out=yr[p], in0=yr[p], scalar=mask_slot[:, bass.ds(j, 1)], in1=bg[p],
                                       op0=ALU.mult, op1=ALU.add).then_inc(s["f_ym"], 1)
                dve.wait_ge(s["f_ym"], j + 1)
                if not (isinstance(k, int) and k == 0):
                    dve.wait_ge(sc[p], k * 16)
                v.tensor_tensor(og[p], yr[p], c_bc[:, :], ALU.add).then_inc(s["f_o"], 1)
            x_low(0, 0)
            x_low(1, 1)
            h_parts(0, 0)

            def step(i):
                x_low(i * 2, 0)
                h_parts(i * 2 - 1, 1)
                result(i * 2 - 2, 0, i - 1)
                x_low(i * 2 + 1, 1)
                h_parts(i * 2, 0)
                result(i * 2 - 1, 1, i - 1)
            step(1)
            with dve.Fori(2, NT // 2) as i:
                step(i)
            h_parts(NT - 1, 1)
            result(NT - 2, 0, NT // 2 - 1)
            result(NT - 1, 1, NT // 2 - 1)


_INS = ["L0_attn_u", "L0_attn_log_lambda", "L0_attn_B_w", "L0_attn_C_w", "L0_attn_D", "L0_ffn_waff",
        "L0_ffn_W1", "L0_ffn_b1", "L0_ffn_W2", "L0_ffn_b2", "L0_ffn_affinity_threshold"]


def kernel(**inputs):
    import numpy as _np
    import concourse.bacc as _bacc
    from concourse.bass_utils import run_bass_kernel_spmd as _run

    nc = _bacc.Bacc("TRN2", target_bir_lowering=False, num_devices=1)
    arrays, args = {}, []
    for name in _INS:
        a = _np.ascontiguousarray(inputs[name])
        if a.ndim == 0:
            a = a.reshape(1)
        arrays[name] = a
        args.append(nc.dram_tensor(name, a.shape, F32, kind="ExternalInput").ap())
    shape = inputs["L0_attn_u"].shape
    out = nc.dram_tensor("out", shape, F32, kind="ExternalOutput").ap()
    rows = [shape[0] * shape[1], shape[2]]
    xn = nc.dram_tensor("xn_rows", rows, F32).ap()
    base = nc.dram_tensor("base_rows", rows, F32).ap()
    moe_ssm_kernel(nc, *args, out, xn, base)
    r = _run(nc, [arrays], core_ids=[0])
    return r.results[0]["out"]
```

```python
import concourse.bass as bass
from concourse import mybir
from contextlib import ExitStack

F32 = mybir.dt.float32
F16 = mybir.dt.float16
I32 = mybir.dt.int32
ACT = mybir.ActivationFunctionType
ALU = mybir.AluOpType
AX = mybir.AxisListType
RMAX = bass.bass_isa.ReduceOp.max

P = 128


def moe_ssm_kernel(nc, u, log_lambda, B_w, C_w, D_w, waff, W1, b1, W2, b2, threshold, out, xn_dram, base_dram):
    B, S, D = u.shape
    N = B_w.shape[0]
    E, _, F = W1.shape
    Q = S // P
    T = B * Q
    TOKENS = B * S
    K = D // P
    C = F // P
    W = 2 * P
    NT = TOKENS // W + E - 1
    NS = 2 * NT
    PAIRS = B // 2
    UW = K * F
    assert N == 64 and B * E == P and K * F == C * D
    EPS = 1e-5
    XS = 2.0 ** 11
    NEAR = -(2.0 ** -25)

    u_q = u.rearrange("b (q p) d -> b p q d", p=P)
    xn_q = xn_dram.rearrange("(b q p) d -> b p q d", p=P, q=Q)
    base_q = base_dram.rearrange("(b q p) d -> b p q d", p=P, q=Q)
    out_rows = out.rearrange("b s d -> (b s) d")
    w1_v = W1.rearrange("e (k p) f -> e p k f", p=P)
    w2_v = W2.rearrange("e (c p) d -> e p c d", p=P)

    with ExitStack() as ctx:
        def sb(name, cols, dt=F32, rows=P):
            return ctx.enter_context(nc.sbuf_tensor(name, [rows, cols], dt))

        def sem(name):
            return ctx.enter_context(nc.semaphore(name))

        def part_(t, off, n):
            return t[:, off:off + n]

        whi = sb("whi", 2 * E * UW, F16)
        wlo = sb("wlo", 2 * E * UW, F16)
        ring = sb("ring", 4 * UW)
        work = sb("work", 10 * Q * D)
        ident = sb("ident", P)
        ones = sb("ones", P)
        iota_f = sb("iota_f", P)
        pcol = sb("pcol", 2)
        bt = sb("bt", K * N)
        wat = sb("wat", K * E)
        ct = sb("ct", D)
        d_bc = sb("d_bc", D)
        c_bc = sb("c_bc", D)
        b1t = sb("b1t", E * C)
        lam = sb("lam", 4)
        small = sb("small", 64)
        lam_c = lam[:, 3:4]
        newt = sb("newt", 2 * Q)
        stats = sb("stats", 2 * Q * 6)
        exp_w = sb("exp_w", 2 * E, I32)
        exp_h = sb("exp_h", E, I32)
        tmp_i = sb("tmp_i", 2 * E, I32)
        wnorm = sb("wnorm", E)
        thr_bc = sb("thr_bc", 1)
        mv_s = sb("mv_s", 2 * 4 * Q)
        rstd_s = sb("rstd_s", 2 * 2 * Q)
        ve_s = sb("ve_s", 2 * 2 * Q)
        ratio_all = sb("ratio_all", T)
        wsum = sb("wsum", 4)
        wmax = sb("wmax", 4)
        scale_w = sb("scale_w", 2 * E)
        inv_in = sb("inv_in", E)
        h_scale = sb("h_scale", E)
        inv_out = sb("inv_out", E)
        idx_x = sb("idx_x", 8, I32)
        idx_b = sb("idx_b", 8, I32)
        bits = sb("bits", 8, I32)
        cnt = sb("cnt", 8)

        mv = [part_(mv_s, n * 4 * Q, 4 * Q) for n in range(2)]
        rstd = [part_(rstd_s, n * 2 * Q, 2 * Q) for n in range(2)]
        ve = [part_(ve_s, n * 2 * Q, 2 * Q) for n in range(2)]
        def part(t, off, n):
            return t[:, off:off + n]
        QD = Q * D
        xb = [part(work, n * QD, QD).rearrange("p (q d) -> p q d", q=Q) for n in range(4)]
        xnb = [part(work, (4 + n) * QD, QD).rearrange("p (q d) -> p q d", q=Q) for n in range(2)]
        xnt = [part(work, (6 + n) * QD, QD).rearrange("p (k s) -> p k s", k=K) for n in range(2)]
        hs = [part(work, 8 * QD + n * S, S) for n in range(2)]
        dxn = part(work, 9 * QD, QD).rearrange("p (q d) -> p q d", q=Q)
        iota_i = part(work, 9 * QD + 3 * D, P).bitcast(I32)
        idx_all = part(work, 9 * QD + P, NS).bitcast(I32)
        mask_slot = part(work, 9 * QD + P + NS, NS)
        tile_expert = part(work, 9 * QD + P + 2 * NS, NT).bitcast(I32)
        gb16 = part(work, 9 * QD + P + 2 * NS + NT, E * C).bitcast(F16)
        ones16 = part(work, 9 * QD + 2 * D, P // 2).bitcast(F16)
        tri16 = part(work, 9 * QD + 2 * D + P // 2, P // 2).bitcast(F16)
        raw = [part(ring, n * UW, UW) for n in range(4)]
        st_b = dxn.rearrange("p q d -> p (q d)")[0:N, 0:D]
        st_c = hs[0][:, 0:K * 2 * N].rearrange("p (k r n) -> p k r n", k=K, r=2)
        st_w = hs[1][0:E, 0:D]
        st_b1 = dxn.rearrange("p q d -> p (q d)")[0:E * C, D:D + P]
        st_b2 = hs[1][0:E, D:2 * D]
        watsq = dxn.rearrange("p q d -> p (q d)")[:, 2 * D:2 * D + K * E]

        TE = T * E
        aff, a_rows, eq_rows = [part(work, n * TE, TE) for n in range(3)]
        oh16 = part(work, 3 * TE, TE // 2).bitcast(F16)
        o = 3 * TE + TE // 2
        (best, rowmax, pos, hi_f, lo_f, tnum, mtok, xnorm, sq0, sq1, ratio) = [part(work, o + n * T, T) for n in range(11)]
        pos_i, hi_i, lo_i = [part(work, o + (11 + n) * T, T).bitcast(I32) for n in range(3)]
        o += 14 * T
        lo16 = part(work, o, T * P // 2).bitcast(F16).rearrange("p (t l) -> p t l", l=P)
        e16 = part(work, o + T * P // 2, T * NS // 2).bitcast(F16).rearrange("p (t j) -> p t j", j=NS)
        diff, cnt_e, scan_e, pos4, den = [part(work, o + n * TE, TE) for n in range(5)]
        v16 = part(ring, 4 * UW - T * NS, T * NS).bitcast(F16).rearrange("p (r t j) -> p r t j", r=2, j=NS)
        g_bc = part(ring, 0, E * D)
        tcmp = part(ring, E * D, NT * E)
        gelu_b = part(ring, E * D + NT * E, E * C)
        HW = C * W
        h32 = part(ring, E * D, HW)
        hpar = [part(ring, E * D + HW, HW), part(ring, E * D + 2 * HW, HW)]
        hhi = [x[:, 0:HW // 2].bitcast(F16) for x in hpar]
        hlo = [x[:, HW // 2:HW].bitcast(F16) for x in hpar]
        xg, bg, og, yr = [[part(work, (2 * m + n) * 2 * D, 2 * D) for n in range(2)] for m in range(4)]
        xhi, xlo = [[part(work, 16 * D + (2 * m + n) * D, D).bitcast(F16).rearrange("p (k t) -> p k t", k=K)
                     for n in range(2)] for m in range(2)]

        def psum(name, cols):
            return ctx.enter_context(nc.psum_tensor(name, [P, cols], F32))
        ps_t = psum("ps_t", 1024)
        ps_bu = psum("ps_bu", 512)
        ps_num = psum("ps_num", 512)
        ps_y = psum("ps_y", 1024)
        ps_s = psum("ps_s", 512)
        ps_g = psum("ps_g", 512)
        ps_h = [ps_t[:, 0:512], ps_t[:, 512:1024], ps_y[:, 0:512], ps_y[:, 512:1024]]
        CQ = C // 4
        QW = CQ * W
        ps_x = [ps_s, ps_g]
        ps_o = [ps_bu, ps_num]

        s = {n: sem(n) for n in (
            "params_in", "consts", "pe_const", "dve_const", "act_const",
            "x_in0", "x_in1", "x_in2", "x_in3", "w_in0", "w_in1", "w_in2", "w_in3",
            "stats", "std", "rstd_ok", "xn_ok", "xt_ok", "xt_out", "num_ok", "bu_ok", "scan_ok", "y_ok",
            "dx_ok", "base_ok", "xn_out0", "xn_out1", "base_out0", "base_out1", "base_out2", "base_out3",
            "wsum_ok", "wmax_ok", "wscale_ok", "whi_ok", "wlo_ok",
            "dve_chain", "r_pe", "r_act", "r_dve", "r_pool", "g_pe", "g_dve",
            "oh_pos", "inv_pe", "idx_ok", "m_ok",
            "gx0", "gx1", "gb0", "gb1", "sc0", "sc1", "ix", "ib",
            "f_xt", "f_xhi", "f_xlo", "f_h", "f_gelu", "f_hhi", "f_hlo", "f_y", "f_yr", "f_ym", "f_o",
            "gates", "cleared", "r_dve2", "r_pool2", "newton", "wchain", "ratio_c")}
        block = ctx.enter_context(nc.Block())
        x_in = [s[f"x_in{n}"] for n in range(4)]
        w_in = [s[f"w_in{n}"] for n in range(4)]
        xn_out = [s[f"xn_out{n}"] for n in range(2)]
        base_out = [s[f"base_out{n}"] for n in range(4)]

        def wait(eng, sm, v):
            if not (isinstance(v, int) and v <= 0):
                eng.wait_ge(sm, v)

        PARAMS = 10 * 16
        PEEL = 4
        assert NT % 2 == 1

        @block.sync
        def _(sp):
            def load(dst, src):
                sp.dma_start(dst, src).then_inc(s["params_in"], 16)
            load(st_b, B_w)
            load(st_c[:, :, 0, :], C_w.rearrange("(k p) n -> p k n", p=P))
            load(st_c[:, :, 1, :], C_w.rearrange("(k p) n -> p k n", p=P))
            load(st_w, waff)
            load(st_b1, b1.rearrange("e (c f) -> (e c) f", f=P))
            load(st_b2, b2)
            load(lam[0:N, 0:1], log_lambda)
            load(lam[N:2 * N, 0:1], log_lambda)
            load(d_bc[:, :], D_w.partition_broadcast(P))
            load(thr_bc[:, :], threshold.partition_broadcast(P))
            for n in range(4):
                sp.dma_start(xb[n], u_q[n]).then_inc(x_in[n], 16)

            def turn(i, last):
                for pr in range(2):
                    for h in range(2):
                        n = 2 * pr + h
                        b = i * 4 + n
                        if not isinstance(b, int):
                            b = sp.snap(b, min_val=0, max_val=B - 1)
                            v1 = sp.snap(i * 4 + n + 1)
                        else:
                            v1 = i * 4 + n + 1
                        sp.wait_ge(s["xn_ok"], v1)
                        sp.dma_start(xn_q[bass.ds(b, 1)].rearrange("a p q d -> (a p) q d"),
                                     xnb[h]).then_inc(xn_out[h], 16)
                    for h in range(2):
                        n = 2 * pr + h
                        b = i * 4 + n
                        if not isinstance(b, int):
                            b = sp.snap(b, min_val=0, max_val=B - 1)
                            v1 = sp.snap(i * 4 + n + 1)
                            v2 = sp.snap(i * 16 + 16)
                        else:
                            v1 = i * 4 + n + 1
                            v2 = i * 16 + 16
                        sp.wait_ge(s["base_ok"], v1)
                        sp.dma_start(base_q[bass.ds(b, 1)].rearrange("a p q d -> (a p) q d"),
                                     xb[n]).then_inc(base_out[n], 16)
                        if not last:
                            b2_ = sp.snap(i * 4 + (n + 4), min_val=0, max_val=B - 1) if not isinstance(b, int) else b + 4
                            sp.wait_ge(base_out[n], v2)
                            sp.dma_start(xb[n], u_q[bass.ds(b2_, 1)].rearrange("a p q d -> (a p) q d")).then_inc(x_in[n], 16)
            turn(0, False)
            with sp.Fori(1, PAIRS // 2 - 1) as i:
                turn(i, False)
            turn(PAIRS // 2 - 1, True)

        @block.gpsimd
        def _(pool):
            g = nc.gpsimd
            link_n = [0]

            def link(ins):
                link_n[0] += 1
                ins.then_inc(s["r_pool"], 1)
                pool.wait_ge(s["r_pool"], link_n[0])
            link(g.memset(ident[:], 1.0))
            link(g.affine_select(out=ident[:], in_=ident[:], compare_op=ALU.is_equal, fill=0.0, base=0,
                                 pattern=[[-1, P]], channel_multiplier=1))
            link(g.memset(ones[:], 1.0))
            link(g.iota(iota_i[:], [[1, P]], base=0, channel_multiplier=0))
            link(g.tensor_copy(iota_f[:], iota_i[:]))
            link(g.iota(iota_i[:, 0:1], [[0, 1]], base=1, channel_multiplier=1))
            g.tensor_copy(pcol[:, 0:1], iota_i[:, 0:1]).then_inc(s["consts"], 1)
            pool.wait_ge(s["consts"], 1)

            def gate(before):
                wait(pool, s["gates"], before)
                g.tensor_tensor(cnt[:, 5:6], ones[:, 0:1], ones[:, 0:1], ALU.add).then_inc(s["gates"], 1)

            def turn(i):
                for pr in range(2):
                    for h in range(2):
                        n = 2 * pr + h
                        uu = i * 4 + n
                        pool.wait_ge(s["wsum_ok"], i * 4 + (n + 1))
                        gate(i * 4 + n)
                        g.partition_all_reduce(wmax[:, n:n + 1], wsum[:, n:n + 1], P,
                                               RMAX).then_inc(s["wmax_ok"], 1)
                    for h in range(2):
                        n = 2 * pr + h
                        bat = i * 4 + n
                        pool.wait_ge(s["xn_ok"], bat + 1)
                        wait(pool, s["dx_ok"], bat * 2)
                        g.tensor_tensor(dxn, xnb[h], d_bc[:].rearrange("p (a d) -> p a d", a=1).to_broadcast([P, Q, D]),
                                        ALU.mult).then_inc(s["dx_ok"], 1)
                        pool.wait_ge(s["dx_ok"], i * 8 + (2 * n + 1))
                        g.tensor_tensor(xb[n], xb[n], dxn, ALU.add).then_inc(s["dx_ok"], 1)
            pool.wait_ge(s["params_in"], PARAMS)
            pool.wait_ge(s["pe_const"], 4)
            turn(0)
            with pool.Fori(1, PAIRS // 2) as i:
                turn(i)

            gx, gb, sc = [s["gx0"], s["gx1"]], [s["gb0"], s["gb1"]], [s["sc0"], s["sc1"]]
            for n in range(2):
                pool.wait_ge(xn_out[n], 16 * (B // 2))
            for n in range(4):
                pool.wait_ge(base_out[n], 16 * (B // 4))
            link(g.tensor_copy(ones16, ones[:]))
            link(g.iota(iota_i[:, 0:T], [[1, Q], [Q, B]], base=0, channel_multiplier=0))
            link(g.tensor_copy(tnum, iota_i[:, 0:T]))
            g.affine_select(out=tri16, in_=ones16, compare_op=ALU.is_gt, fill=0.0, base=0,
                            pattern=[[1, P]], channel_multiplier=-1).then_inc(s["r_pool2"], 1)
            pool.wait_ge(s["r_dve"], 2)
            g.partition_all_reduce(small[:, 56:64], small[:, 48:56], P, RMAX).then_inc(s["r_pool2"], 1)
            pool.wait_ge(s["idx_ok"], 1)
            for p in range(2):
                g.memset(xg[p], 0.0)
                g.memset(bg[p], 0.0).then_inc(s["cleared"], 1)
            pool.wait_ge(s["cleared"], 2)

            bound = pool.to_reg(TOKENS - 1)

            def is_tile(j):
                return not isinstance(j, int) or 0 <= j < NT

            def step(m, r, gate_no):
                t_out, t_base = m - 5, m - 3
                if is_tile(m):
                    wait(pool, s["f_xt"], m - 1)
                    gate(gate_no)
                    g.tensor_copy(idx_x[:, 2 * r:2 * r + 2], idx_all[:, bass.ds(m * 2, 2)]).then_inc(s["ix"], 1)
                    pool.wait_ge(s["ix"], m + 1)
                    gate(gate_no + 1)
                    gate_no = gate_no + 2
                    for h in range(2):
                        g.indirect_dma_start(out=xg[r % 2][:, h * D:(h + 1) * D], out_offset=None, in_=xn_dram,
                                             in_offset=bass.IndirectOffsetOnAxis(
                                                 ap=idx_x[:, 2 * r + h:2 * r + h + 1], axis=0),
                                             bounds_check=bound, oob_is_err=False).then_inc(gx[r % 2], 16)
                rb = (r + 1) % 4
                if is_tile(t_out):
                    pool.wait_ge(s["f_o"], t_out + 1)
                    gate(gate_no)
                    gate_no = gate_no + 1
                if is_tile(t_base):
                    g.tensor_copy(idx_b[:, 2 * rb:2 * rb + 2], idx_all[:, bass.ds(t_base * 2, 2)]).then_inc(s["ib"], 1)
                if is_tile(t_out):
                    ro = (r + 3) % 4
                    for h in range(2):
                        g.indirect_dma_start(out=out_rows,
                                             out_offset=bass.IndirectOffsetOnAxis(
                                                 ap=idx_b[:, 2 * ro + h:2 * ro + h + 1], axis=0),
                                             in_=og[ro % 2][:, h * D:(h + 1) * D], in_offset=None,
                                             bounds_check=bound, oob_is_err=False).then_inc(sc[ro % 2], 16)
                if is_tile(t_base):
                    pool.wait_ge(s["ib"], t_base + 1)
                    gate(gate_no)
                    gate_no = gate_no + 1
                    for h in range(2):
                        g.indirect_dma_start(out=bg[rb % 2][:, h * D:(h + 1) * D], out_offset=None, in_=base_dram,
                                             in_offset=bass.IndirectOffsetOnAxis(
                                                 ap=idx_b[:, 2 * rb + h:2 * rb + h + 1], axis=0),
                                             bounds_check=bound, oob_is_err=False).then_inc(gb[rb % 2], 16)
                return gate_no
            gates = B
            for m in range(8):
                gates = step(m, m % 4, gates)
            with pool.Fori(2, NT // 4) as i:
                for r in range(4):
                    step(i * 4 + r, r, i * 16 + (gates - 32 + 4 * r))
            gates += 4 * (NT // 4 * 4 - 8)
            for m in range(NT // 4 * 4, NT + 5):
                gates = step(m, m % 4, gates)
            for p in range(2):
                pool.wait_ge(sc[p], 32 * ((NT + 1 - p) // 2))

        @block.scalar
        def _(act):
            a = nc.scalar

            def wload(e, w, slot):
                v = (w1_v if w == 0 else w2_v)[bass.ds(e, 1)].rearrange("a p k f -> (a p) k f")
                dst = raw[slot].rearrange("p (k f) -> p k f", k=K if w == 0 else C)
                act.dma_start(dst, v).then_inc(w_in[slot], 16)
            for n in range(4):
                wload(n // 2, n % 2, n)
            act.wait_ge(s["params_in"], PARAMS)
            a.activation(lam[:, 1:2], lam[:, 0:1], ACT.Exp, scale=-1.0).then_inc(s["act_const"], 1)
            act.wait_ge(s["pe_const"], 5)
            a.activation(small[:, 0:E], ps_g[:, 0:E], ACT.Sqrt).then_inc(s["act_const"], 1)

            def turn(i, last):
                for pr in range(2):
                    pair = i * 2 + pr
                    act.wait_ge(s["stats"], pair + 1)
                    a.activation(rstd[pr], ve[pr], ACT.Sqrt).then_inc(s["std"], 1)
                    for w in range(2):
                        n = 2 * pr + w
                        uu = i * 4 + n
                        act.wait_ge(w_in[n], i * 16 + 16)
                        a.activation(whi[:, bass.ds(uu * UW, UW)], raw[n], ACT.Abs,
                                     accum_out=wsum[:, n:n + 1]).then_inc(s["wsum_ok"], 1)
                    for h in range(2):
                        for k in range(K):
                            m = (2 * pr + h) * K + k
                            act.wait_ge(s["xt_ok"], i * (4 * K) + (m + 1))
                            if not (isinstance(i, int) and i == 0 and pr == 0):
                                act.wait_ge(s["bu_ok"], pair)
                            a.copy(xnt[h][:, k, :], ps_t[:, k * S:(k + 1) * S]).then_inc(s["xt_out"], 1)
                    for w in range(2):
                        n = 2 * pr + w
                        uu = i * 4 + n
                        act.wait_ge(s["wscale_ok"], uu + 1)
                        a.activation(whi[:, bass.ds(uu * UW, UW)], raw[n], ACT.Copy,
                                     scale=scale_w[:, bass.ds(uu, 1)]).then_inc(s["whi_ok"], 1)
                    if not last:
                        for w in range(2):
                            n = 2 * pr + w
                            e2 = act.snap(i * 2 + (pr + 2), min_val=0, max_val=E - 1) if not isinstance(i, int) else i * 2 + pr + 2
                            act.wait_ge(s["wlo_ok"], i * 4 + (n + 1))
                            wload(e2, w, n)
            turn(0, False)
            with act.Fori(1, PAIRS // 2 - 1) as i:
                turn(i, False)
            turn(PAIRS // 2 - 1, True)

            act.wait_ge(s["r_dve"], 1)
            a.activation(sq0, xnorm, ACT.Sqrt).then_inc(s["r_act"], 1)
            act.wait_ge(s["wlo_ok"], 2 * E)
            a.activation(gelu_b, b1t[:, :], ACT.Gelu).then_inc(s["r_act"], 1)
            act.wait_ge(s["r_dve"], 4)
            a.activation(small[:, 20:21], small[:, 19:20], ACT.Exp, scale=-1.0).then_inc(s["r_act"], 1)

            def split_x(j, p):
                act.wait_ge(s["f_xt"], j + 1)
                if not (isinstance(j, int) and j < 2):
                    act.wait_ge(s["f_h"], (j - 1) * 4)
                a.activation(xhi[p].rearrange("p k t -> p (k t)"), ps_x[p][:, 0:K * W], ACT.Copy,
                             scale=XS).then_inc(s["f_xhi"], 1)

            def hidden(j):
                e = act.value_load(tile_expert[0:1, bass.ds(j, 1)], min_val=0, max_val=E - 1)
                for qt in range(4):
                    act.wait_ge(s["f_h"], j * 4 + (1 + qt))
                    if not (isinstance(j, int) and j < 1):
                        act.wait_ge(s["f_hlo"], (j - 1) * 4 + (1 + qt))
                    for c in range(qt * CQ, (qt + 1) * CQ):
                        ins = a.activation(h32[:, c * W:(c + 1) * W], ps_h[qt][:, c % CQ * W:(c % CQ + 1) * W], ACT.Gelu,
                                           bias=b1t[:, bass.ds(e * C + c, 1)], scale=inv_in[:, bass.ds(e, 1)])
                    ins.then_inc(s["f_gelu"], 1)
            act.wait_ge(s["idx_ok"], 1)

            def step(j, p):
                split_x(j + 1, 1 - p)
                hidden(j)
            split_x(0, 0)
            for j in range(PEEL):
                step(j, j % 2)
            with act.Fori(PEEL // 2, NT // 2) as i:
                for p in range(2):
                    step(i * 2 + p, p)
            hidden(NT - 1)

        @block.tensor
        def _(pe):
            t = nc.tensor
            pe.wait_ge(s["params_in"], PARAMS)
            pe.wait_ge(s["consts"], 1)
            for k in range(K):
                t.transpose(ps_s[:, k * N:(k + 1) * N], st_b[:, k * P:(k + 1) * P], ident[0:N, 0:N])
            last = t.transpose(ps_s[:, 128 + 0:128 + P], st_c[:, 0, :, :].rearrange("p r n -> p (r n)"), ident[:])
            last = t.transpose(ps_s[:, 128 + P:128 + 2 * P], st_c[:, 1, :, :].rearrange("p r n -> p (r n)"), ident[:])
            last.then_inc(s["pe_const"], 1)
            for k in range(K):
                last = t.transpose(ps_s[:, 384 + k * E:384 + (k + 1) * E], st_w[:, k * P:(k + 1) * P], ident[0:E, 0:E])
            last.then_inc(s["pe_const"], 1)
            t.transpose(ps_g[:, 64:64 + E * C], st_b1, ident[0:E * C, 0:E * C]).then_inc(s["pe_const"], 1)
            t.matmul(ps_g[:, 128:128 + D], ones[0:E, :], st_b2, start=True, stop=True).then_inc(s["pe_const"], 1)
            pe.wait_ge(s["dve_const"], 1)
            for k in range(K):
                last = t.matmul(ps_g[:, 0:E], ones[:], watsq[:, k * E:(k + 1) * E], start=(k == 0), stop=(k == K - 1))
            last.then_inc(s["pe_const"], 1)

            def turn(i):
                for pr in range(2):
                    pair = i * 2 + pr
                    for h in range(2):
                        bat = i * 4 + (2 * pr + h)
                        pe.wait_ge(s["xn_ok"], bat + 1)
                        for k in range(K):
                            if not (isinstance(i, int) and i == 0 and pr == 0 and h == 0):
                                pe.wait_ge(s["xt_out"], bat * K + (k + 1 - K))
                            for q in range(Q):
                                last = t.transpose(ps_t[:, k * S + q * P:k * S + (q + 1) * P],
                                                   xnb[h][:, q, k * P:(k + 1) * P], ident[:])
                            last.then_inc(s["xt_ok"], 1)
                    for h in range(2):
                        bat = i * 4 + (2 * pr + h)
                        pe.wait_ge(s["xt_out"], bat * K + K)
                        for q in range(Q):
                            for k in range(K):
                                last = t.matmul(ps_num[:, bass.ds(bat * E + q * B * E, E)],
                                                xnt[h][:, k, q * P:(q + 1) * P], wat[:, k * E:(k + 1) * E],
                                                start=(k == 0), stop=(k == K - 1))
                        last.then_inc(s["num_ok"], 1)
                        if h == 0 and not (isinstance(i, int) and i == 0 and pr == 0):
                            pe.wait_ge(s["scan_ok"], pair)
                        for k in range(K):
                            last = t.matmul(ps_bu[h * N:(h + 1) * N, :], bt[:, k * N:(k + 1) * N], xnt[h][:, k, :],
                                            start=(k == 0), stop=(k == K - 1))
                    last.then_inc(s["bu_ok"], 1)
                    pe.wait_ge(s["scan_ok"], pair + 1)
                    for h in range(2):
                        bat = i * 4 + (2 * pr + h)
                        if not (isinstance(i, int) and i == 0 and pr == 0 and h == 0):
                            pe.wait_ge(s["base_ok"], bat)
                        for q in range(Q):
                            last = t.matmul(ps_y[:, q * D:(q + 1) * D], hs[pr][h * N:(h + 1) * N, q * P:(q + 1) * P],
                                            ct[h * N:(h + 1) * N, :], start=True, stop=True)
                        last.then_inc(s["y_ok"], 1)
            pe.wait_ge(s["dve_const"], 2)
            turn(0)
            with pe.Fori(1, PAIRS // 2) as i:
                turn(i)

            pe.wait_ge(s["oh_pos"], 1)
            pe.wait_ge(s["r_pool2"], 1)
            t.matmul(ps_s[:, 0:TE], tri16, oh16, start=True, stop=True)
            t.matmul(ps_bu[:, 0:TE], ones16, oh16, start=True, stop=True).then_inc(s["r_pe"], 1)
            pe.wait_ge(s["g_dve"], 1)
            for e in range(E):
                if e >= 2:
                    pe.wait_ge(s["g_dve"], e)
                dst = (ps_g, ps_num)[e % 2][:, 0:D]
                for c in range(C):
                    n = e * C + c
                    w2h = whi[:, (2 * e + 1) * UW + c * D:(2 * e + 1) * UW + (c + 1) * D]
                    w2l = wlo[:, (2 * e + 1) * UW + c * D:(2 * e + 1) * UW + (c + 1) * D]
                    gh = gb16[:, n:n + 1].to_broadcast([P, P])
                    gl = gb16[:, E * C + n:E * C + n + 1].to_broadcast([P, P])
                    t.matmul(dst, gh, w2h, start=(c == 0), stop=False)
                    t.matmul(dst, gh, w2l, start=False, stop=False)
                    last = t.matmul(dst, gl, w2h, start=False, stop=(c == C - 1))
                last.then_inc(s["g_pe"], 1)
            pe.wait_ge(s["r_dve"], 3)
            for q in range(Q):
                last = t.transpose(ps_t[:, q * P:(q + 1) * P], aff[:, q * P:(q + 1) * P], ident[:])
            last.then_inc(s["r_pe"], 1)
            t.matmul(ps_y[:, 0:1], ones[:], small[:, 16:17], start=True, stop=True).then_inc(s["r_pe"], 1)
            pe.wait_ge(s["oh_pos"], 2)
            for tt in range(T):
                last = t.matmul(ps_s[:, 0:2 * NS], lo16[:, tt, :], v16[:, :, tt, :], start=(tt == 0), stop=(tt == T - 1))
            last.then_inc(s["inv_pe"], 1)
            pe.wait_ge(s["oh_pos"], 3)
            for q in range(Q):
                last = t.transpose(ps_t[:, S + q * P:S + (q + 1) * P], eq_rows[:, q * P:(q + 1) * P], ident[:])
            last.then_inc(s["r_pe"], 1)
            pe.wait_ge(s["oh_pos"], 4)
            for tt in range(T):
                last = t.matmul(ps_s[:, 256:256 + NS], lo16[:, tt, :], v16[:, 0, tt, :], start=(tt == 0), stop=(tt == T - 1))
            last.then_inc(s["inv_pe"], 1)

            gx = [s["gx0"], s["gx1"]]

            def rows_t(j, p, k):
                pe.wait_ge(gx[p], k * 32 + 32)
                if not (isinstance(j, int) and j < 2):
                    pe.wait_ge(s["f_xlo"], j - 1)
                for kk in range(K):
                    for h in range(2):
                        last = t.transpose(ps_x[p][:, kk * W + h * P:kk * W + (h + 1) * P],
                                           xg[p][:, h * D + kk * P:h * D + (kk + 1) * P], ident[:])
                last.then_inc(s["f_xt"], 1)

            def up(j, p):
                e = pe.value_load(tile_expert[0:1, bass.ds(j, 1)], min_val=0, max_val=E - 1)
                w0 = pe.snap(e * (2 * UW))
                pe.wait_ge(s["f_xlo"], j + 1)
                for qt in range(4):
                    if not (isinstance(j, int) and j < 1):
                        pe.wait_ge(s["f_gelu"], (j - 1) * 4 + (1 + qt))
                    for c in range(qt * CQ, (qt + 1) * CQ):
                        dst = ps_h[qt][:, c % CQ * W:(c % CQ + 1) * W]
                        for k in range(K):
                            wh = whi[:, bass.ds(w0 + (k * F + c * P), P)]
                            wl = wlo[:, bass.ds(w0 + (k * F + c * P), P)]
                            t.matmul(dst, wh, xhi[p][:, k, :], start=(k == 0), stop=False)
                            t.matmul(dst, wh, xlo[p][:, k, :], start=False, stop=False)
                            last = t.matmul(dst, wl, xhi[p][:, k, :], start=False, stop=(k == K - 1))
                    last.then_inc(s["f_h"], 1)

            def down(j, p):
                e = pe.value_load(tile_expert[0:1, bass.ds(j, 1)], min_val=0, max_val=E - 1)
                w0 = pe.snap(e * (2 * UW) + UW)
                if not (isinstance(j, int) and j < 2):
                    pe.wait_ge(s["f_yr"], j - 1)
                for h in range(2):
                    for c in range(C):
                        if h == 0 and c % CQ == 0:
                            pe.wait_ge(s["f_hlo"], j * 4 + (1 + c // CQ))
                        wh = whi[:, bass.ds(w0 + c * D, D)]
                        wl = wlo[:, bass.ds(w0 + c * D, D)]
                        dst = ps_o[p][:, h * D:(h + 1) * D]
                        hh = hhi[p][:, c * W + h * P:c * W + (h + 1) * P]
                        hl = hlo[p][:, c * W + h * P:c * W + (h + 1) * P]
                        t.matmul(dst, hh, wh, start=(c == 0), stop=False)
                        t.matmul(dst, hh, wl, start=False, stop=False)
                        last = t.matmul(dst, hl, wh, start=False, stop=(c == C - 1))
                last.then_inc(s["f_y"], 1)
            pe.wait_ge(s["idx_ok"], 1)

            def step(j, p, k):
                rows_t(j + 1, 1 - p, k + p)
                up(j, p)
                if not (isinstance(j, int) and j < 1):
                    down(j - 1, 1 - p)
            rows_t(0, 0, 0)
            for j in range(PEEL):
                step(j, j % 2, j // 2)
            with pe.Fori(PEEL // 2, NT // 2) as i:
                for p in range(2):
                    step(i * 2 + p, p, i)
            up(NT - 1, 0)
            down(NT - 2, 1)
            down(NT - 1, 0)

        @block.vector
        def _(dve):
            v = nc.vector
            link_n = [0]

            def link(ins):
                link_n[0] += 1
                ins.then_inc(s["dve_chain"], 1)
                dve.wait_ge(s["dve_chain"], link_n[0])

            def power_of_two(dst, src, n, exps):
                link(v.tensor_scalar(exps, src.bitcast(I32), 23, None, ALU.logical_shift_right))
                link(v.tensor_scalar(exps, exps, -1.0, 268.0, ALU.mult, ALU.add))
                link(v.tensor_scalar(exps, exps, 250.0, 4.0, ALU.min, ALU.max))
                link(v.tensor_scalar(dst.bitcast(I32), exps, 23, None, ALU.logical_shift_left))

            dve.wait_ge(s["pe_const"], 2)
            v.tensor_copy(bt[:, :], ps_s[:, 0:K * N])
            v.tensor_copy(ct[:, :], ps_s[:, 128:128 + D])
            link(v.tensor_copy(wat[:, :], ps_s[:, 384:384 + K * E]))
            v.tensor_tensor(watsq, wat[:, :], wat[:, :], ALU.mult).then_inc(s["dve_const"], 1)
            dve.wait_ge(s["pe_const"], 5)
            dve.wait_ge(s["act_const"], 1)
            link(v.tensor_scalar(lam[:, 2:3], lam[:, 1:2], 1.0, None, ALU.add))
            link(v.reciprocal(lam[:, 3:4], lam[:, 2:3]))
            dve.wait_ge(s["act_const"], 2)
            v.tensor_copy(b1t[:, :], ps_g[:, 64:64 + E * C])
            v.tensor_copy(c_bc[:, :], ps_g[:, 128:128 + D])
            link(v.tensor_scalar(small[:, 8:16], small[:, 0:8], 1e-30, None, ALU.max))
            link(v.reciprocal(small[:, 24:32], small[:, 8:16]))
            link(v.tensor_tensor(small[:, 32:40], small[:, 24:32], ps_g[:, 0:E], ALU.mult))
            link(v.tensor_tensor(small[:, 8:16], small[:, 0:8], small[:, 32:40], ALU.add))
            link(v.tensor_scalar(wnorm[:, :], small[:, 8:16], 0.5, None, ALU.mult))
            v.memset(cnt[:, 0:1], 0.0).then_inc(s["dve_const"], 1)

            def stats_of(pair, nb, first):
                pr = nb // 2
                for h in range(2):
                    n = nb + h
                    if isinstance(pair, int):
                        dve.wait_ge(x_in[n], 16 * (pair // 2 + 1))
                    else:
                        dve.wait_ge(x_in[n], first)
                    for q in range(Q):
                        c = (h * Q + q) * 6
                        last = v.bn_stats(stats[:, c:c + 6], xb[n][:, q, :])
                last.then_inc(s["r_dve2"], 1)
                dve.wait_ge(s["r_dve2"], pair * 2 + 1)
                v.memset(cnt[:, 4:5], 0.0)
                for c in range(2 * Q):
                    last = v.bn_aggr(mv[pr][:, 2 * c:2 * c + 2], stats[:, c * 6:(c + 1) * 6])
                last.then_inc(s["r_dve2"], 1)
                dve.wait_ge(s["r_dve2"], pair * 2 + 2)
                v.tensor_scalar(ve[pr], mv[pr].rearrange("p (t m) -> p t m", m=2)[:, :, 1],
                                EPS, None, ALU.add).then_inc(s["stats"], 1)

            def rstd_of(pair, pr):
                r_ = rstd[pr]
                v_ = ve[pr]
                nw = s["newton"]
                dve.wait_ge(s["std"], pair + 1)
                v.reciprocal(r_, r_).then_inc(nw, 1)
                dve.wait_ge(nw, pair * 5 + 1)
                v.tensor_tensor(newt[:, :], r_, r_, ALU.mult).then_inc(nw, 1)
                dve.wait_ge(nw, pair * 5 + 2)
                v.tensor_tensor(newt[:, :], newt[:, :], v_, ALU.mult).then_inc(nw, 1)
                dve.wait_ge(nw, pair * 5 + 3)
                v.tensor_scalar(newt[:, :], newt[:, :], -0.5, 1.5, ALU.mult, ALU.add).then_inc(nw, 1)
                dve.wait_ge(nw, pair * 5 + 4)
                v.tensor_tensor(r_, r_, newt[:, :], ALU.mult).then_inc(nw, 1)
                dve.wait_ge(nw, pair * 5 + 5)
                v.tensor_tensor(newt[:, :], mv[pr].rearrange("p (t m) -> p t m", m=2)[:, :, 1], r_,
                                ALU.mult).then_inc(s["ratio_c"], 1)
                dve.wait_ge(s["ratio_c"], pair + 1)
                v.tensor_tensor(ratio_all[:, bass.ds(pair * (2 * Q), 2 * Q)], newt[:, :], r_, ALU.mult)

            def turn(i, last_turn):
                for pr in range(2):
                    pair = i * 2 + pr
                    for h in range(2):
                        n = 2 * pr + h
                        bat = i * 4 + n
                        if not (isinstance(i, int) and i == 0 and pr == 0):
                            dve.wait_ge(s["xt_ok"], (bat - 1) * K)
                            dve.wait_ge(s["dx_ok"], (bat - 2) * 2 + 1)
                            dve.wait_ge(xn_out[h], pair * 16)
                        for q in range(Q):
                            tt = h * Q + q
                            last = v.tensor_scalar(xnb[h][:, q, :], xb[n][:, q, :], mv[pr][:, 2 * tt:2 * tt + 1],
                                                   rstd[pr][:, tt:tt + 1], ALU.subtract, ALU.mult)
                        last.then_inc(s["xn_ok"], 1)
                    final = last_turn and pr == 1
                    if not final:
                        stats_of(pair + 1, 2 * (1 - pr), i * 16 + 16 * (1 + pr))
                    for w in range(2):
                        uu = i * 4 + (2 * pr + w)
                        ws = s["wchain"]
                        dve.wait_ge(s["wmax_ok"], uu + 1)
                        ex = exp_w[:, bass.ds(uu, 1)]
                        v.tensor_scalar(ex, wmax[:, 2 * pr + w:2 * pr + w + 1].bitcast(I32), 23, None,
                                        ALU.logical_shift_right).then_inc(ws, 1)
                        dve.wait_ge(ws, uu * 3 + 1)
                        v.tensor_scalar(ex, ex, -1.0, 268.0, ALU.mult, ALU.add).then_inc(ws, 1)
                        dve.wait_ge(ws, uu * 3 + 2)
                        v.tensor_scalar(ex, ex, 250.0, 4.0, ALU.min, ALU.max).then_inc(ws, 1)
                        dve.wait_ge(ws, uu * 3 + 3)
                        v.tensor_scalar(scale_w[:, bass.ds(uu, 1)].bitcast(I32), ex, 23, None,
                                        ALU.logical_shift_left).then_inc(s["wscale_ok"], 1)
                    for w in range(2):
                        n = 2 * pr + w
                        uu = i * 4 + n
                        dve.wait_ge(s["whi_ok"], uu + 1)
                        v.scalar_tensor_tensor(out=wlo[:, bass.ds(uu * UW, UW)], in0=raw[n],
                                               scalar=scale_w[:, bass.ds(uu, 1)], in1=whi[:, bass.ds(uu * UW, UW)],
                                               op0=ALU.mult, op1=ALU.subtract).then_inc(s["wlo_ok"], 1)
                    if not final:
                        rstd_of(pair + 1, 1 - pr)
                    dve.wait_ge(s["bu_ok"], pair + 1)
                    v.tensor_tensor_scan(hs[pr], lam_c.to_broadcast([P, S]), ps_bu[:, :], 0.0, ALU.mult,
                                         ALU.add).then_inc(s["scan_ok"], 1)
                    for h in range(2):
                        n = 2 * pr + h
                        bat = i * 4 + n
                        dve.wait_ge(s["y_ok"], bat + 1)
                        dve.wait_ge(s["dx_ok"], bat * 2 + 2)
                        xf = xb[n].rearrange("p q d -> p (q d)")
                        v.tensor_tensor(xf, ps_y[:, :], xf, ALU.add).then_inc(s["base_ok"], 1)
            stats_of(0, 0, None)
            rstd_of(0, 0)
            turn(0, False)
            with dve.Fori(1, PAIRS // 2 - 1) as i:
                turn(i, False)
            turn(PAIRS // 2 - 1, True)

            for n in range(4):
                dve.wait_ge(base_out[n], 16 * (B // 4))
            for n in range(2):
                dve.wait_ge(xn_out[n], 16 * (B // 2))
            dve.wait_ge(s["num_ok"], B)
            def te(x):
                return x.rearrange("p (t e) -> p t e", e=E)
            def bt_(x):
                return x.rearrange("p (t a) -> p t a", a=1).to_broadcast([P, T, E])
            def be_(x):
                return x.rearrange("p (a e) -> p a e", a=1).to_broadcast([P, T, E])
            link(v.tensor_copy(xnorm.rearrange("p (q b) -> p q b", q=Q), ratio_all[:, :].rearrange("p (b q) -> p q b", q=Q)))
            v.tensor_scalar(cnt[:, 1:2], cnt[:, 0:1], 1.0, None, ALU.add).then_inc(s["r_dve"], 1)
            dve.wait_ge(s["r_act"], 1)
            link(v.tensor_scalar(sq1, sq0, 1e-30, None, ALU.max))
            link(v.reciprocal(ratio, sq1))
            link(v.tensor_tensor(sq1, ratio, xnorm, ALU.mult))
            link(v.tensor_tensor(ratio, sq1, sq0, ALU.add))
            link(v.tensor_scalar(xnorm, ratio, 0.5 * float(D) ** 0.5, None, ALU.mult))
            link(v.tensor_tensor(te(den), bt_(xnorm), be_(wnorm[:, :]), ALU.mult))
            link(v.tensor_scalar(den, den, 1e-9, None, ALU.add))
            link(v.reciprocal(diff, den))
            link(v.tensor_tensor(aff, ps_num[:, 0:TE], diff, ALU.mult))
            link(v.tensor_reduce(rowmax, te(aff), AX.X, ALU.max))
            link(v.tensor_tensor(te(diff), te(aff), bt_(rowmax), ALU.subtract))
            link(v.tensor_scalar(small[:, 40:48], iota_f[:, 0:E], -1.0, float(E), ALU.mult, ALU.add))
            link(v.scalar_tensor_tensor(out=te(den), in0=te(diff), scalar=NEAR, in1=be_(small[:, 40:48]),
                                        op0=ALU.is_ge, op1=ALU.mult))
            link(v.tensor_reduce(best, te(den), AX.X, ALU.max))
            v.tensor_tensor(te(oh16), be_(small[:, 40:48]), bt_(best), ALU.is_equal).then_inc(s["oh_pos"], 1)

            link(v.tensor_reduce(small[:, 48:56], b1t[:, :].rearrange("p (e c) -> p e c", c=C), AX.X, ALU.max,
                                 apply_absolute_value=True))
            v.tensor_scalar(cnt[:, 1:2], cnt[:, 0:1], 1.0, None, ALU.add).then_inc(s["r_dve"], 1)
            dve.wait_ge(s["r_pool2"], 2)
            ew = exp_w[:, :].rearrange("p (e w) -> p e w", w=2)
            link(v.tensor_scalar(tmp_i[:, 0:E], ew[:, :, 0], -1.0, 254.0 - 11.0, ALU.mult, ALU.add))
            link(v.tensor_scalar(tmp_i[:, 0:E], tmp_i[:, 0:E], 1.0, None, ALU.max))
            link(v.tensor_scalar(inv_in[:, :].bitcast(I32), tmp_i[:, 0:E], 23, None, ALU.logical_shift_left))
            link(v.scalar_tensor_tensor(out=small[:, 48:56],
                                        in0=inv_in[:, :], scalar=float(D) * 2.0 ** 15 * XS,
                                        in1=small[:, 56:64], op0=ALU.mult, op1=ALU.add))
            power_of_two(h_scale[:, :], small[:, 48:56], E, exp_h[:, :])
            link(v.tensor_tensor(tmp_i[:, 0:E], ew[:, :, 1], exp_h[:, :], ALU.add) if False else
                 v.scalar_tensor_tensor(out=tmp_i[:, 0:E], in0=ew[:, :, 1], scalar=-1.0, in1=exp_h[:, :],
                                        op0=ALU.mult, op1=ALU.subtract))
            link(v.tensor_scalar(tmp_i[:, 0:E], tmp_i[:, 0:E], 381.0, None, ALU.add))
            link(v.tensor_scalar(tmp_i[:, 0:E], tmp_i[:, 0:E], 1.0, 254.0, ALU.max, ALU.min))
            link(v.tensor_scalar(inv_out[:, :].bitcast(I32), tmp_i[:, 0:E], 23, None, ALU.logical_shift_left))
            dve.wait_ge(s["r_act"], 2)
            gv = gelu_b.rearrange("p (e c) -> p e c", c=C)
            hb = h_scale[:, :].rearrange("p (e a) -> p e a", a=1).to_broadcast([P, E, C])
            link(v.tensor_tensor(gv, gv, hb, ALU.mult))
            link(v.tensor_copy(gb16[:, 0:E * C], gelu_b))
            v.tensor_tensor(gb16[:, E * C:2 * E * C], gelu_b, gb16[:, 0:E * C], ALU.subtract).then_inc(s["g_dve"], 1)

            dve.wait_ge(s["r_pe"], 1)
            link(v.tensor_copy(cnt_e.rearrange("p (e t) -> p t e", e=E), te(ps_bu[:, 0:TE])))
            ce = cnt_e.rearrange("p (e t) -> p e t", e=E)
            link(v.tensor_tensor_scan(scan_e, ones[:, 0:1].to_broadcast([P, TE]), cnt_e, 0.0, ALU.mult, ALU.add))
            link(v.tensor_tensor(scan_e, scan_e, cnt_e, ALU.subtract))
            n_e, tiles_e, t_incl, adj = small[:, 0:8], small[:, 8:16], small[:, 24:32], small[:, 32:40]
            link(v.tensor_reduce(n_e, ce, AX.X, ALU.add))
            link(v.tensor_scalar(sq0, iota_f[:, 0:T], float(W), None, ALU.mult))
            link(v.tensor_tensor(diff.rearrange("p (e t) -> p e t", e=E),
                                 n_e.rearrange("p (e a) -> p e a", a=1).to_broadcast([P, E, T]),
                                 sq0.rearrange("p (a t) -> p a t", a=1).to_broadcast([P, E, T]), ALU.is_gt))
            link(v.tensor_reduce(tiles_e, diff.rearrange("p (e t) -> p e t", e=E), AX.X, ALU.add))
            link(v.tensor_tensor_scan(t_incl, ones[:, 0:E], tiles_e, 0.0, ALU.mult, ALU.add))
            link(v.tensor_tensor(adj, t_incl, tiles_e, ALU.subtract))
            link(v.tensor_tensor_scan(tiles_e, ones[:, 0:E], n_e, 0.0, ALU.mult, ALU.add))
            link(v.tensor_tensor(tiles_e, tiles_e, n_e, ALU.subtract))
            link(v.scalar_tensor_tensor(out=adj, in0=adj, scalar=float(W), in1=tiles_e, op0=ALU.mult, op1=ALU.subtract))
            link(v.tensor_tensor(scan_e.rearrange("p (e t) -> p e t", e=E), scan_e.rearrange("p (e t) -> p e t", e=E),
                                 adj.rearrange("p (e a) -> p e a", a=1).to_broadcast([P, E, T]), ALU.add))
            link(v.tensor_tensor(te(pos4), te(ps_s[:, 0:TE]), scan_e.rearrange("p (e t) -> p t e", e=E), ALU.add))
            link(v.tensor_tensor(pos4, pos4, oh16, ALU.mult))
            link(v.tensor_reduce(pos, te(pos4), AX.X, ALU.add))
            link(v.tensor_copy(pos_i, pos))
            link(v.tensor_scalar(hi_i, pos_i, 7, None, ALU.logical_shift_right))
            link(v.tensor_scalar(lo_i, pos_i, P - 1, None, ALU.bitwise_and))
            link(v.tensor_copy(hi_f, hi_i))
            link(v.tensor_copy(lo_f, lo_i))
            tc = tcmp.rearrange("p (j e) -> p j e", e=E)
            link(v.tensor_tensor(tc, iota_f[:, 0:NT].rearrange("p (j a) -> p j a", a=1).to_broadcast([P, NT, E]),
                                 t_incl.rearrange("p (a e) -> p a e", a=1).to_broadcast([P, NT, E]), ALU.is_ge))
            te_f = mask_slot[:, 0:NT]
            link(v.tensor_reduce(te_f, tc, AX.X, ALU.add))
            link(v.tensor_scalar(te_f, te_f, float(E - 1), None, ALU.min))
            link(v.tensor_copy(tile_expert, te_f))

            link(v.tensor_reduce(small[:, 16:17], aff, AX.X, ALU.add))
            v.tensor_scalar(cnt[:, 1:2], cnt[:, 0:1], 1.0, None, ALU.add).then_inc(s["r_dve"], 1)

            v.tensor_tensor(lo16, iota_f[:, :].rearrange("p (a l) -> p a l", a=1).to_broadcast([P, T, P]),
                            lo_f.rearrange("p (t a) -> p t a", a=1).to_broadcast([P, T, P]), ALU.is_equal)
            link(v.tensor_tensor(e16, iota_f[:, 0:NS].rearrange("p (a j) -> p a j", a=1).to_broadcast([P, T, NS]),
                                 hi_f.rearrange("p (t a) -> p t a", a=1).to_broadcast([P, T, NS]), ALU.is_equal))
            v.tensor_scalar(v16[:, 0], e16, pcol[:, 0:1], None, ALU.mult)
            v.tensor_tensor(v16[:, 1], e16, tnum.rearrange("p (t a) -> p t a", a=1).to_broadcast([P, T, NS]),
                            ALU.mult).then_inc(s["oh_pos"], 1)
            for e in range(E):
                dve.wait_ge(s["g_pe"], e + 1)
                v.tensor_scalar(g_bc[:, e * D:(e + 1) * D], (ps_g, ps_num)[e % 2][:, 0:D],
                                inv_out[:, e:e + 1], None, ALU.mult).then_inc(s["g_dve"], 1)
                dve.wait_ge(s["g_dve"], e + 2)
                link(v.tensor_tensor(c_bc[:, :], c_bc[:, :], g_bc[:, e * D:(e + 1) * D], ALU.add))
            dve.wait_ge(s["inv_pe"], 1)
            iv = mask_slot
            link(v.tensor_scalar(iv, ps_s[:, 0:NS], 0.5, float(4 * TOKENS), ALU.is_lt, ALU.mult))
            link(v.tensor_tensor(iv, ps_s[:, 0:NS], iv, ALU.add))
            link(v.scalar_tensor_tensor(out=iv, in0=ps_s[:, NS:2 * NS], scalar=float(P), in1=iv, op0=ALU.mult, op1=ALU.add))
            link(v.tensor_scalar(iv, iv, -1.0, None, ALU.add))
            link(v.tensor_copy(idx_all, iv))

            dve.wait_ge(s["r_pe"], 3)
            z, cap = small[:, 19:20], small[:, 21:22]
            link(v.tensor_scalar(small[:, 18:19], ps_y[:, 0:1], 1.0 / (TOKENS * E), None, ALU.mult))
            link(v.tensor_tensor(z, small[:, 18:19], thr_bc[:, :], ALU.subtract))
            v.tensor_scalar(cnt[:, 1:2], cnt[:, 0:1], 1.0, None, ALU.add).then_inc(s["r_dve"], 1)
            dve.wait_ge(s["r_act"], 3)
            link(v.tensor_scalar(small[:, 17:18], small[:, 20:21], 1.0, None, ALU.add))
            link(v.reciprocal(small[:, 18:19], small[:, 17:18]))
            link(v.tensor_scalar(cap, small[:, 18:19], float(S), None, ALU.mult))
            link(v.tensor_copy(tmp_i[:, 0:1], cap))
            link(v.tensor_copy(small[:, 17:18], tmp_i[:, 0:1]))
            link(v.tensor_tensor(small[:, 18:19], small[:, 17:18], cap, ALU.is_gt))
            link(v.tensor_tensor(cap, small[:, 17:18], small[:, 18:19], ALU.subtract))
            link(v.tensor_scalar(cap, cap, 4.0, float(S), ALU.max, ALU.min))

            link(v.tensor_copy(a_rows, ps_t[:, 0:S]))
            sign, kth, kneg = small[:, 22:23], small[:, 23:24], small[:, 24:25]
            link(v.tensor_scalar(eq_rows, a_rows, 0.0, 0.0, ALU.is_ge, ALU.add, accum_out=cnt[:, 2:3]))
            link(v.tensor_tensor(kneg, cnt[:, 2:3], cap, ALU.is_lt))
            link(v.tensor_scalar(sign, kneg, -2.0, 1.0, ALU.mult, ALU.add))
            link(v.tensor_scalar(small[:, 25:26], cap, -2.0, float(S + 1), ALU.mult, ALU.add))
            link(v.scalar_tensor_tensor(out=kth, in0=small[:, 25:26], scalar=kneg, in1=cap, op0=ALU.mult, op1=ALU.add))
            srch = aff
            link(v.tensor_scalar(srch, a_rows, sign, None, ALU.mult))
            cand, tb = bits[:, 0:1], bits[:, 1:2]
            link(v.memset(cand, 1 << 30))
            for bit in range(30, -1, -1):
                link(v.tensor_scalar(eq_rows, srch, cand.bitcast(F32), 0.0, ALU.is_ge, ALU.add, accum_out=cnt[:, 2:3]))
                link(v.tensor_scalar(tb, cnt[:, 2:3], kth, float(1 << bit), ALU.is_lt, ALU.mult))
                if bit:
                    link(v.scalar_tensor_tensor(out=cand, in0=tb, scalar=1 << (bit - 1), in1=cand,
                                                op0=ALU.bitwise_or, op1=ALU.bitwise_xor))
                else:
                    link(v.tensor_tensor(cand, tb, cand, ALU.bitwise_xor))
            thr = small[:, 26:27]
            link(v.tensor_tensor(thr, cand.bitcast(F32), sign, ALU.mult))
            gt = aff
            link(v.tensor_scalar(gt, a_rows, thr, 0.0, ALU.is_gt, ALU.add, accum_out=cnt[:, 3:4]))
            link(v.tensor_tensor(small[:, 27:28], cap, cnt[:, 3:4], ALU.subtract))
            link(v.tensor_scalar(eq_rows, a_rows, thr, None, ALU.is_equal))
            link(v.tensor_tensor_scan(a_rows, ones[:, 0:1].to_broadcast([P, S]), eq_rows, 0.0, ALU.mult, ALU.add))
            link(v.scalar_tensor_tensor(out=eq_rows, in0=a_rows, scalar=small[:, 27:28], in1=eq_rows,
                                        op0=ALU.is_le, op1=ALU.mult))
            v.tensor_tensor(eq_rows, eq_rows, gt, ALU.add).then_inc(s["oh_pos"], 1)
            dve.wait_ge(s["r_pe"], 4)
            link(v.tensor_tensor(aff, ps_t[:, S:2 * S], oh16, ALU.mult))
            link(v.tensor_reduce(mtok, te(aff), AX.X, ALU.add))
            v.tensor_tensor(v16[:, 0], e16, mtok.rearrange("p (t a) -> p t a", a=1).to_broadcast([P, T, NS]),
                            ALU.mult).then_inc(s["oh_pos"], 1)
            dve.wait_ge(s["inv_pe"], 2)
            v.tensor_copy(mask_slot, ps_s[:, 256:256 + NS]).then_inc(s["idx_ok"], 1)

            gb = [s["gb0"], s["gb1"]]
            sc = [s["sc0"], s["sc1"]]

            def x_low(j, p):
                dve.wait_ge(s["f_xhi"], j + 1)
                v.scalar_tensor_tensor(out=xlo[p].rearrange("p k t -> p (k t)"), in0=ps_x[p][:, 0:K * W], scalar=XS,
                                       in1=xhi[p].rearrange("p k t -> p (k t)"), op0=ALU.mult,
                                       op1=ALU.subtract).then_inc(s["f_xlo"], 1)

            def h_parts(j, p):
                e = dve.value_load(tile_expert[0:1, bass.ds(j, 1)], min_val=0, max_val=E - 1)
                for qt in range(4):
                    cs = slice(qt * QW, (qt + 1) * QW)
                    dve.wait_ge(s["f_gelu"], j * 4 + (1 + qt))
                    if qt == 0 and not (isinstance(j, int) and j < 2):
                        dve.wait_ge(s["f_y"], j - 1)
                    v.tensor_scalar(hhi[p][:, cs], h32[:, cs], h_scale[:, bass.ds(e, 1)], None,
                                    ALU.mult).then_inc(s["f_hhi"], 1)
                    dve.wait_ge(s["f_hhi"], j * 4 + (1 + qt))
                    v.scalar_tensor_tensor(out=hlo[p][:, cs], in0=h32[:, cs], scalar=h_scale[:, bass.ds(e, 1)],
                                           in1=hhi[p][:, cs], op0=ALU.mult, op1=ALU.subtract).then_inc(s["f_hlo"], 1)

            def result(j, p, k):
                e = dve.value_load(tile_expert[0:1, bass.ds(j, 1)], min_val=0, max_val=E - 1)
                dve.wait_ge(s["f_y"], j + 1)
                halves = [slice(h * D, (h + 1) * D) for h in range(2)]
                for hs_ in halves:
                    last = v.scalar_tensor_tensor(out=yr[p][:, hs_], in0=ps_o[p][:, hs_], scalar=inv_out[:, bass.ds(e, 1)],
                                                  in1=g_bc[:, bass.ds(e * D, D)], op0=ALU.mult, op1=ALU.subtract)
                last.then_inc(s["f_yr"], 1)
                dve.wait_ge(s["f_yr"], j + 1)
                dve.wait_ge(gb[p], k * 32 + 32)
                for h, hs_ in enumerate(halves):
                    last = v.scalar_tensor_tensor(out=yr[p][:, hs_], in0=yr[p][:, hs_],
                                                  scalar=mask_slot[:, bass.ds(j * 2 + h, 1)], in1=bg[p][:, hs_],
                                                  op0=ALU.mult, op1=ALU.add)
                last.then_inc(s["f_ym"], 1)
                dve.wait_ge(s["f_ym"], j + 1)
                if not (isinstance(k, int) and k == 0):
                    dve.wait_ge(sc[p], k * 32)
                v.tensor_tensor(og[p].rearrange("p (h d) -> p h d", h=2), yr[p].rearrange("p (h d) -> p h d", h=2),
                                c_bc[:, :].rearrange("p (a d) -> p a d", a=1).to_broadcast([P, 2, D]),
                                ALU.add).then_inc(s["f_o"], 1)

            def step(j, p, k):
                x_low(j + 1, 1 - p)
                h_parts(j, p)
                if not (isinstance(j, int) and j < 1):
                    result(j - 1, 1 - p, k - 1 + p)
            x_low(0, 0)
            for j in range(PEEL):
                step(j, j % 2, j // 2)
            with dve.Fori(PEEL // 2, NT // 2) as i:
                for p in range(2):
                    step(i * 2 + p, p, i)
            h_parts(NT - 1, 0)
            result(NT - 2, 1, NT // 2 - 1)
            result(NT - 1, 0, NT // 2)


_INS = ["L0_attn_u", "L0_attn_log_lambda", "L0_attn_B_w", "L0_attn_C_w", "L0_attn_D", "L0_ffn_waff",
        "L0_ffn_W1", "L0_ffn_b1", "L0_ffn_W2", "L0_ffn_b2", "L0_ffn_affinity_threshold"]


def kernel(**inputs):
    import numpy as _np
    import concourse.bacc as _bacc
    from concourse.bass_utils import run_bass_kernel_spmd as _run

    nc = _bacc.Bacc("TRN2", target_bir_lowering=False, num_devices=1)
    arrays, args = {}, []
    for name in _INS:
        a = _np.ascontiguousarray(inputs[name])
        if a.ndim == 0:
            a = a.reshape(1)
        arrays[name] = a
        args.append(nc.dram_tensor(name, a.shape, F32, kind="ExternalInput").ap())
    shape = inputs["L0_attn_u"].shape
    out = nc.dram_tensor("out", shape, F32, kind="ExternalOutput").ap()
    rows = [shape[0] * shape[1], shape[2]]
    xn = nc.dram_tensor("xn_rows", rows, F32).ap()
    base = nc.dram_tensor("base_rows", rows, F32).ap()
    moe_ssm_kernel(nc, *args, out, xn, base)
    r = _run(nc, [arrays], core_ids=[0])
    return r.results[0]["out"]
```

```python
import concourse.bass as bass
from concourse import mybir
from contextlib import ExitStack

F32 = mybir.dt.float32
F16 = mybir.dt.float16
I32 = mybir.dt.int32
ACT = mybir.ActivationFunctionType
ALU = mybir.AluOpType
AX = mybir.AxisListType
RMAX = bass.bass_isa.ReduceOp.max

P = 128


def moe_ssm_kernel(nc, u, log_lambda, B_w, C_w, D_w, waff, W1, b1, W2, b2, threshold, out, xn_dram, base_dram, num_dram):
    B, S, D = u.shape
    N = B_w.shape[0]
    E, _, F = W1.shape
    Q = S // P
    T = B * Q
    TOKENS = B * S
    K = D // P
    C = F // P
    W = 2 * P
    NT = TOKENS // W + E - 1
    NS = 2 * NT
    PAIRS = B // 2
    UW = K * F
    assert N == 64 and B * E == P and K * F == C * D
    EPS = 1e-5
    XS = 2.0 ** 11
    NEAR = -(2.0 ** -25)

    u_q = u.rearrange("b (q p) d -> b p q d", p=P)
    xn_q = xn_dram.rearrange("(b q p) d -> b p q d", p=P, q=Q)
    base_q = base_dram.rearrange("(b q p) d -> b p q d", p=P, q=Q)
    num_q = num_dram.rearrange("(b e) s -> b e s", e=E)
    out_rows = out.rearrange("b s d -> (b s) d")
    w1_v = W1.rearrange("e (k p) f -> e p k f", p=P)
    w2_v = W2.rearrange("e (c p) d -> e p c d", p=P)

    with ExitStack() as ctx:
        def sb(name, cols, dt=F32, rows=P):
            return ctx.enter_context(nc.sbuf_tensor(name, [rows, cols], dt))

        def sem(name):
            return ctx.enter_context(nc.semaphore(name))

        def part(t, off, n):
            return t[:, off:off + n]

        whi = sb("whi", 2 * E * UW, F16)
        wlo = sb("wlo", 2 * E * UW, F16)
        ring = sb("ring", 4 * UW)
        work = sb("work", 10 * Q * D)
        ident = sb("ident", P)
        ones = sb("ones", P)
        iota_f = sb("iota_f", P)
        pcol = sb("pcol", 2)
        NE = N + E
        bwt = sb("bwt", K * NE)
        bwk = bwt[:, :].rearrange("p (k n) -> p k n", k=K)
        ct = sb("ct", D)
        d_bc = sb("d_bc", D)
        c_bc = sb("c_bc", D)
        b1t = sb("b1t", E * C)
        lam = sb("lam", 4)
        small = sb("small", 64)
        lam_c = lam[:, 3:4]
        newt = sb("newt", 2 * Q)
        stats = sb("stats", 2 * Q * 6)
        exp_w = sb("exp_w", 2 * E, I32)
        exp_h = sb("exp_h", E, I32)
        tmp_i = sb("tmp_i", 2 * E, I32)
        wnorm = sb("wnorm", E)
        thr_bc = sb("thr_bc", 1)
        mv_s = sb("mv_s", 2 * 4 * Q)
        rstd_s = sb("rstd_s", 2 * 2 * Q)
        ve_s = sb("ve_s", 2 * 2 * Q)
        ratio_all = sb("ratio_all", T)
        wsum = sb("wsum", 4)
        wmax = sb("wmax", 4)
        scale_w = sb("scale_w", 2 * E)
        inv_in = sb("inv_in", E)
        h_scale = sb("h_scale", E)
        inv_out = sb("inv_out", E)
        idx_x = sb("idx_x", 8, I32)
        idx_b = sb("idx_b", 8, I32)
        bits = sb("bits", 8, I32)
        search = sb("search", 8)
        cnt = sb("cnt", 8)

        mv = [part(mv_s, n * 4 * Q, 4 * Q) for n in range(2)]
        rstd = [part(rstd_s, n * 2 * Q, 2 * Q) for n in range(2)]
        ve = [part(ve_s, n * 2 * Q, 2 * Q) for n in range(2)]
        QD = Q * D
        xb = [part(work, n * QD, QD).rearrange("p (q d) -> p q d", q=Q) for n in range(4)]
        xnb = [part(work, (4 + n) * QD, QD).rearrange("p (q d) -> p q d", q=Q) for n in range(2)]
        xnt = [part(work, (6 + n) * QD, QD).rearrange("p (k s) -> p k s", k=K) for n in range(2)]
        hs = [part(work, 8 * QD + n * S, S) for n in range(2)]
        dxn = part(work, 9 * QD, QD).rearrange("p (q d) -> p q d", q=Q)
        iota_i = part(work, 9 * QD + 3 * D, P).bitcast(I32)
        num_rows = part(work, 6 * QD, S)
        idx_all = part(work, 9 * QD + P, NS).bitcast(I32)
        mask_slot = part(work, 9 * QD + P + NS, NS)
        tile_expert = part(work, 9 * QD + P + 2 * NS, NT).bitcast(I32)
        gb16 = part(work, 9 * QD + P + 2 * NS + NT, E * C).bitcast(F16)
        ones16 = part(work, 9 * QD + 2 * D, P // 2).bitcast(F16)
        tri16 = part(work, 9 * QD + 2 * D + P // 2, P // 2).bitcast(F16)
        neg16 = part(work, 9 * QD + 2 * D + P, P // 2).bitcast(F16)
        raw = [part(ring, n * UW, UW) for n in range(4)]
        st_b = dxn.rearrange("p q d -> p (q d)")[0:N, 0:D]
        st_c = hs[0][:, 0:K * 2 * N].rearrange("p (k r n) -> p k r n", k=K, r=2)
        st_w = hs[1][0:E, 0:D]
        st_b1 = dxn.rearrange("p q d -> p (q d)")[0:E * C, D:D + P]
        st_b2 = hs[1][0:E, D:2 * D]
        watsq = dxn.rearrange("p q d -> p (q d)")[:, 2 * D:2 * D + K * E]

        TE = T * E
        aff, a_rows, eq_rows = [part(work, n * TE, TE) for n in range(3)]
        oh16 = part(work, 3 * TE, TE // 2).bitcast(F16)
        o = 3 * TE + TE // 2
        (best, rowmax, pos, hi_f, lo_f, tnum, mtok) = [part(work, o + n * T, T) for n in range(7)]
        pos_i, hi_i, lo_i = [part(work, o + (7 + n) * T, T).bitcast(I32) for n in range(3)]
        o += 14 * T
        lo16 = part(work, o, T * P // 2).bitcast(F16).rearrange("p (t l) -> p t l", l=P)
        e16 = part(work, o + T * P // 2, T * NS // 2).bitcast(F16).rearrange("p (t j) -> p t j", j=NS)
        diff, cnt_e, scan_e, pos4 = [part(work, o + n * TE, TE) for n in range(4)]
        den, rden = [part(ring, n * TE, TE) for n in range(2)]
        xnorm, sq0, sq1, ratio = [part(ring, 2 * TE + n * T, T) for n in range(4)]
        v16 = part(ring, 4 * UW - T * NS, T * NS).bitcast(F16).rearrange("p (r t j) -> p r t j", r=2, j=NS)
        g_bc = part(ring, 0, E * D)
        tcmp = part(ring, E * D, NT * E)
        gelu_b = part(ring, 2 * TE + 4 * T, E * C)
        key_hi = part(ring, E * D + NT * E, S)
        signs = part(ring, E * D + NT * E + S, S // 2).bitcast(F16)
        HW = C * W
        h32 = part(ring, E * D, HW)
        hpar = [part(ring, E * D + HW, HW), part(work, 12 * D, HW)]
        hhi = [x[:, 0:HW // 2].bitcast(F16) for x in hpar]
        hlo = [x[:, HW // 2:HW].bitcast(F16) for x in hpar]
        bg, og, yr = [[part(work, (2 * m + n) * 2 * D, 2 * D) for n in range(2)] for m in range(3)]
        o = E * D + 2 * HW
        xg = [part(ring, o + n * 2 * D, 2 * D) for n in range(2)]
        xhi, xlo = [[part(ring, o + 4 * D + (2 * m + n) * D, D).bitcast(F16).rearrange("p (k t) -> p k t", k=K)
                     for n in range(2)] for m in range(2)]

        def g_bank(e):
            return (ps_g[:, 0:2 * D], ps_y[:, 0:2 * D], ps_y[:, 2 * D:4 * D], ps_num[:, 0:2 * D])[e // 2][:, e % 2 * D:(e % 2 + 1) * D]

        def psum(name, cols):
            return ctx.enter_context(nc.psum_tensor(name, [P, cols], F32))
        ps_t = psum("ps_t", 1024)
        ps_bu = psum("ps_bu", 512)
        ps_num = psum("ps_num", 512)
        ps_y = psum("ps_y", 1024)
        ps_s = psum("ps_s", 512)
        ps_g = psum("ps_g", 512)
        bu_bank = [ps_bu, ps_num]

        def y_bank(h, q):
            if h == 0:
                return ps_y[:, q * D:(q + 1) * D]
            return (ps_s, ps_g)[q // 2][:, q % 2 * D:(q % 2 + 1) * D]
        ps_h = [ps_t[:, 0:512], ps_t[:, 512:1024], ps_y[:, 0:512], ps_y[:, 512:1024]]
        CQ = C // 4
        QW = CQ * W
        ps_x = [ps_s, ps_g]
        ps_o = [ps_bu, ps_num]

        s = {n: sem(n) for n in (
            "params_in", "consts", "pe_const", "dve_const", "act_const",
            "x_in0", "x_in1", "x_in2", "x_in3", "w_in0", "w_in1", "w_in2", "w_in3",
            "stats", "std", "xn_ok", "xt_ok", "xt_out", "num_ok", "bu_ok", "scan_ok", "y_ok",
            "dx_ok", "base_ok", "xn_out0", "xn_out1", "base_out0", "base_out1", "base_out2", "base_out3",
            "wsum_ok", "wmax_ok", "wscale_ok", "whi_ok", "wlo_ok",
            "dve_chain", "r_pool", "b1_max", "b1_bound", "xnorm_ok", "xroot_ok", "gelu_ok", "gb_ok",
            "g_pe", "g_out", "aff_ok", "aff_t", "oh_ok", "tri_ok", "counts_ok", "z_ok", "exp_ok", "search",
            "key_hi_ok", "hi_found", "key_lo_ok", "lo_found", "e_ok", "tile_no_ok", "planes_ok", "inverse_ok", "idx_ok",
            "kept_ok", "kept_t", "mtok_ok", "kept_e_ok", "kept_inv", "mask_ok",
            "gx0", "gx1", "gb0", "gb1", "sc0", "sc1", "ix", "ib",
            "f_xt", "f_xhi", "f_xlo", "f_h", "f_gelu", "f_hhi", "f_hlo", "f_y", "f_yr", "f_ym", "f_o",
            "gates", "num_out0", "num_out1", "num_back", "num_t", "cleared", "r_dve2", "newton", "wchain", "ratio_c", "ratios_ok")}
        block = ctx.enter_context(nc.Block())
        x_in = [s[f"x_in{n}"] for n in range(4)]
        w_in = [s[f"w_in{n}"] for n in range(4)]
        xn_out = [s[f"xn_out{n}"] for n in range(2)]
        base_out = [s[f"base_out{n}"] for n in range(4)]

        def wait(eng, sm, v):
            if not (isinstance(v, int) and v <= 0):
                eng.wait_ge(sm, v)

        PARAMS = 10 * 16
        PEEL = 4
        assert NT % 2 == 1

        @block.sync
        def _(sp):
            def load(dst, src):
                sp.dma_start(dst, src).then_inc(s["params_in"], 16)
            load(st_b, B_w)
            load(st_c[:, :, 0, :], C_w.rearrange("(k p) n -> p k n", p=P))
            load(st_c[:, :, 1, :], C_w.rearrange("(k p) n -> p k n", p=P))
            load(st_w, waff)
            load(st_b1, b1.rearrange("e (c f) -> (e c) f", f=P))
            load(st_b2, b2)
            load(lam[0:N, 0:1], log_lambda)
            load(lam[N:2 * N, 0:1], log_lambda)
            load(d_bc[:, :], D_w.partition_broadcast(P))
            load(thr_bc[:, :], threshold.partition_broadcast(P))
            for n in range(2, 4):
                sp.dma_start(xb[n], u_q[n]).then_inc(x_in[n], 16)

            def number(v, top):
                return v if isinstance(v, int) else sp.snap(v, min_val=0, max_val=top)

            def rows_out(bat, n):
                b = number(bat, B - 1)
                done = bat + 1 if isinstance(bat, int) else sp.snap(bat + 1)
                sp.wait_ge(s["xn_ok"], done)
                sp.dma_start(xn_q[bass.ds(b, 1)].rearrange("a p q d -> (a p) q d"), xnb[n % 2]).then_inc(xn_out[n % 2], 16)

            def base_rows_out(bat, n):
                b = number(bat, B - 1)
                done = bat + 1 if isinstance(bat, int) else sp.snap(bat + 1)
                sp.wait_ge(s["base_ok"], done)
                sp.dma_start(base_q[bass.ds(b, 1)].rearrange("a p q d -> (a p) q d"), xb[n]).then_inc(base_out[n], 16)

            def rows_in(bat, n, left):
                b = number(bat, B - 1)
                left = left if isinstance(left, int) else sp.snap(left)
                sp.wait_ge(base_out[n], left)
                sp.dma_start(xb[n], u_q[bass.ds(b, 1)].rearrange("a p q d -> (a p) q d")).then_inc(x_in[n], 16)

            def num_out(bat, h):
                b = number(bat, B - 1)
                done = bat + 1 if isinstance(bat, int) else sp.snap(bat + 1)
                sp.wait_ge(s["num_ok"], done)
                sp.dma_start(num_q[bass.ds(b, 1)].rearrange("a e s -> (a e) s"), hs[h][N:NE, :]).then_inc(s[f"num_out{h}"], 16)

            def weights_in(e, w, n, cut):
                e_ = number(e, E - 1)
                done = cut if isinstance(cut, int) else sp.snap(cut)
                sp.wait_ge(s["wlo_ok"], done)
                src = (w1_v if w == 0 else w2_v)[bass.ds(e_, 1)].rearrange("a p k f -> (a p) k f")
                sp.dma_start(raw[n].rearrange("p (k f) -> p k f", k=K if w == 0 else C), src).then_inc(w_in[n], 16)

            def turn(i, last=False):
                for pr in range(2):
                    for h in range(2):
                        rows_out(i * 4 + (2 * pr + h), 2 * pr + h)
                    if not last:
                        for w in range(2):
                            weights_in(i * 2 + (pr + 2), w, 2 * pr + w, i * 4 + (2 * pr + w + 1))
                    for h in range(2):
                        num_out(i * 4 + (2 * pr + h), h)
                    if last and pr == 1:
                        for h in range(2):
                            sp.wait_ge(s[f"num_out{h}"], 16 * (B // 2))
                        sp.wait_ge(s["bu_ok"], B)
                        sp.dma_start(num_rows, num_dram).then_inc(s["num_back"], 16)
                    for h in range(2):
                        base_rows_out(i * 4 + (2 * pr + h), 2 * pr + h)
                    if not last:
                        for h in range(2):
                            rows_in(i * 4 + (2 * pr + 4 + h), 2 * pr + h, i * 16 + 16)
            turn(0)
            with sp.Fori(1, PAIRS // 2 - 1) as i:
                turn(i)
            turn(PAIRS // 2 - 1, last=True)

        @block.gpsimd
        def _(pool):
            g = nc.gpsimd
            link_n = [0]

            def link(ins):
                link_n[0] += 1
                ins.then_inc(s["r_pool"], 1)
                pool.wait_ge(s["r_pool"], link_n[0])
            link(g.memset(ident[:], 1.0))
            link(g.affine_select(out=ident[:], in_=ident[:], compare_op=ALU.is_equal, fill=0.0, base=0,
                                 pattern=[[-1, P]], channel_multiplier=1))
            link(g.memset(ones[:], 1.0))
            link(g.iota(iota_i[:], [[1, P]], base=0, channel_multiplier=0))
            link(g.tensor_copy(iota_f[:], iota_i[:]))
            link(g.iota(iota_i[:, 0:1], [[0, 1]], base=1, channel_multiplier=1))
            g.tensor_copy(pcol[:, 0:1], iota_i[:, 0:1]).then_inc(s["consts"], 1)
            pool.wait_ge(s["consts"], 1)

            def gate(before):
                wait(pool, s["gates"], before)
                g.tensor_tensor(cnt[:, 5:6], ones[:, 0:1], ones[:, 0:1], ALU.add).then_inc(s["gates"], 1)

            def weight_bound(uu, n):
                pool.wait_ge(s["wsum_ok"], uu + 1)
                gate(uu)
                g.partition_all_reduce(wmax[:, n:n + 1], wsum[:, n:n + 1], P, RMAX).then_inc(s["wmax_ok"], 1)

            def turn(i, last=False):
                for pr in range(2):
                    for h in range(2):
                        n = 2 * pr + h
                        bat = i * 4 + n
                        pool.wait_ge(s["xn_ok"], bat + 1)
                        wait(pool, s["dx_ok"], bat * 2)
                        g.tensor_tensor(dxn, xnb[h], d_bc[:].rearrange("p (a d) -> p a d", a=1).to_broadcast([P, Q, D]),
                                        ALU.mult).then_inc(s["dx_ok"], 1)
                        pool.wait_ge(s["dx_ok"], i * 8 + (2 * n + 1))
                        g.tensor_tensor(xb[n], xb[n], dxn, ALU.add).then_inc(s["dx_ok"], 1)
                    if not (last and pr == 1):
                        for w in range(2):
                            weight_bound(i * 4 + (2 * pr + 2 + w), 2 - 2 * pr + w)
            pool.wait_ge(s["params_in"], PARAMS)
            pool.wait_ge(s["pe_const"], 4)
            pool.wait_ge(s["b1_max"], 1)
            g.partition_all_reduce(small[:, 56:64], small[:, 48:56], P, RMAX).then_inc(s["b1_bound"], 1)
            for w in range(2):
                weight_bound(w, w)
            turn(0)
            with pool.Fori(1, PAIRS // 2 - 1) as i:
                turn(i)
            turn(PAIRS // 2 - 1, last=True)

            gx, gb, sc = [s["gx0"], s["gx1"]], [s["gb0"], s["gb1"]], [s["sc0"], s["sc1"]]
            for n in range(2):
                pool.wait_ge(xn_out[n], 16 * (B // 2))
            for n in range(4):
                pool.wait_ge(base_out[n], 16 * (B // 4))
            link(g.tensor_copy(ones16, ones[:]))
            link(g.iota(iota_i[:, 0:T], [[1, Q], [Q, B]], base=0, channel_multiplier=0))
            link(g.tensor_copy(tnum, iota_i[:, 0:T]))
            link(g.tensor_scalar(neg16, ones[:], -1.0, None, ALU.mult))
            g.affine_select(out=tri16, in_=neg16, compare_op=ALU.is_ge, fill=0.0, base=0,
                            pattern=[[-1, P]], channel_multiplier=1).then_inc(s["tri_ok"], 1)
            for quarter in range(4):
                pool.wait_ge(s["e_ok"], 1 + quarter // 2)
                ts = slice(quarter * T // 4, (quarter + 1) * T // 4)
                g.tensor_tensor(v16[:, 1, ts, :], e16[:, ts, :],
                                tnum[:, ts].rearrange("p (t a) -> p t a", a=1).to_broadcast([P, T // 4, NS]),
                                ALU.mult).then_inc(s["tile_no_ok"], 1)
            pool.wait_ge(s["inverse_ok"], 1)
            for p in range(2):
                g.memset(xg[p], 0.0).then_inc(s["cleared"], 1)
            pool.wait_ge(s["cleared"], 2)
            pool.wait_ge(s["idx_ok"], 1)

            bound = pool.to_reg(TOKENS - 1)

            def is_tile(j):
                return not isinstance(j, int) or 0 <= j < NT

            def step(m, r, gate_no):
                t_out, t_base = m - 5, m - 3
                if is_tile(m):
                    wait(pool, s["f_xt"], m - 1)
                    gate(gate_no)
                    g.tensor_copy(idx_x[:, 2 * r:2 * r + 2], idx_all[:, bass.ds(m * 2, 2)]).then_inc(s["ix"], 1)
                    pool.wait_ge(s["ix"], m + 1)
                    gate(gate_no + 1)
                    gate_no = gate_no + 2
                    for h in range(2):
                        g.indirect_dma_start(out=xg[r % 2][:, h * D:(h + 1) * D], out_offset=None, in_=xn_dram,
                                             in_offset=bass.IndirectOffsetOnAxis(
                                                 ap=idx_x[:, 2 * r + h:2 * r + h + 1], axis=0),
                                             bounds_check=bound, oob_is_err=False).then_inc(gx[r % 2], 16)
                rb = (r + 1) % 4
                if is_tile(t_out):
                    pool.wait_ge(s["f_o"], t_out + 1)
                    gate(gate_no)
                    gate_no = gate_no + 1
                if isinstance(m, int) and m == 3:
                    pool.wait_ge(s["mtok_ok"], 1)
                    g.tensor_tensor(e16, e16, mtok.rearrange("p (t a) -> p t a", a=1).to_broadcast([P, T, NS]),
                                    ALU.mult).then_inc(s["kept_e_ok"], 1)
                    pool.wait_ge(s["mask_ok"], 1)
                    for p in range(2):
                        g.memset(bg[p], 0.0).then_inc(s["cleared"], 1)
                    pool.wait_ge(s["cleared"], 4)
                if is_tile(t_base):
                    g.tensor_copy(idx_b[:, 2 * rb:2 * rb + 2], idx_all[:, bass.ds(t_base * 2, 2)]).then_inc(s["ib"], 1)
                if is_tile(t_out):
                    ro = (r + 3) % 4
                    for h in range(2):
                        g.indirect_dma_start(out=out_rows,
                                             out_offset=bass.IndirectOffsetOnAxis(
                                                 ap=idx_b[:, 2 * ro + h:2 * ro + h + 1], axis=0),
                                             in_=og[ro % 2][:, h * D:(h + 1) * D], in_offset=None,
                                             bounds_check=bound, oob_is_err=False).then_inc(sc[ro % 2], 16)
                if is_tile(t_base):
                    pool.wait_ge(s["ib"], t_base + 1)
                    gate(gate_no)
                    gate_no = gate_no + 1
                    for h in range(2):
                        g.indirect_dma_start(out=bg[rb % 2][:, h * D:(h + 1) * D], out_offset=None, in_=base_dram,
                                             in_offset=bass.IndirectOffsetOnAxis(
                                                 ap=idx_b[:, 2 * rb + h:2 * rb + h + 1], axis=0),
                                             bounds_check=bound, oob_is_err=False).then_inc(gb[rb % 2], 16)
                return gate_no
            gates = B
            for m in range(8):
                gates = step(m, m % 4, gates)
            with pool.Fori(2, NT // 4) as i:
                for r in range(4):
                    step(i * 4 + r, r, i * 16 + (gates - 32 + 4 * r))
            gates += 4 * (NT // 4 * 4 - 8)
            for m in range(NT // 4 * 4, NT + 5):
                gates = step(m, m % 4, gates)
            for p in range(2):
                pool.wait_ge(sc[p], 32 * ((NT + 1 - p) // 2))

        @block.scalar
        def _(act):
            a = nc.scalar

            def first_weights(e, w, slot):
                v = (w1_v if w == 0 else w2_v)[bass.ds(e, 1)].rearrange("a p k f -> (a p) k f")
                dst = raw[slot].rearrange("p (k f) -> p k f", k=K if w == 0 else C)
                act.dma_start(dst, v).then_inc(w_in[slot], 16)
            for n in range(2):
                act.dma_start(xb[n], u_q[n]).then_inc(x_in[n], 16)
            act.wait_ge(s["params_in"], PARAMS)
            for n in range(4):
                first_weights(n // 2, n % 2, n)
            a.activation(lam[:, 1:2], lam[:, 0:1], ACT.Exp, scale=-1.0).then_inc(s["act_const"], 1)
            act.wait_ge(s["pe_const"], 5)
            a.activation(small[:, 0:E], ps_g[:, 0:E], ACT.Sqrt).then_inc(s["act_const"], 1)

            def deviation(pair, pr):
                act.wait_ge(s["stats"], pair + 1)
                a.activation(rstd[pr], ve[pr], ACT.Sqrt).then_inc(s["std"], 1)

            def high_parts(pair, pr):
                act.wait_ge(s["wscale_ok"], pair + 1)
                for w in range(2):
                    uu = pair * 2 + w
                    a.activation(whi[:, bass.ds(uu * UW, UW)], raw[2 * pr + w], ACT.Copy,
                                 scale=scale_w[:, bass.ds(uu, 1)]).then_inc(s["whi_ok"], 1)

            def weight_sums(pair, pr, loads):
                for w in range(2):
                    n = 2 * pr + w
                    act.wait_ge(w_in[n], loads)
                    a.activation(whi[:, bass.ds((pair * 2 + w) * UW, UW)], raw[n], ACT.Abs,
                                 accum_out=wsum[:, n:n + 1]).then_inc(s["wsum_ok"], 1)

            def turn(i, first=False, last=False):
                for pr in range(2):
                    pair = i * 2 + pr
                    if not (first and pr == 0):
                        high_parts(pair, pr)
                    for h in range(2):
                        for k in range(K):
                            m = (2 * pr + h) * K + k
                            act.wait_ge(s["xt_ok"], i * (4 * K) + (m + 1))
                            if not (first and pr == 0):
                                act.wait_ge(s["bu_ok"], i * 4 + (2 * pr + h - 1))
                            a.copy(xnt[h][:, k, :], ps_t[:, k * S:(k + 1) * S]).then_inc(s["xt_out"], 1)
                    if first and pr == 0:
                        high_parts(pair, pr)
                    if not (last and pr == 1):
                        weight_sums(pair + 1, 1 - pr, i * 16 + 16 * (1 + pr))
                    if last and pr == 1:
                        act.wait_ge(s["xnorm_ok"], 1)
                        a.activation(sq0, xnorm, ACT.Sqrt).then_inc(s["xroot_ok"], 1)
                    for h in range(2):
                        act.wait_ge(s["bu_ok"], i * 4 + (2 * pr + h + 1))
                        if not (first and pr == 0):
                            act.wait_ge(s[f"num_out{h}"], i * 32 + 16 * pr)
                        a.copy(hs[h][N:NE, :], bu_bank[h][N:NE, :]).then_inc(s["num_ok"], 1)
                    if not (last and pr == 1):
                        deviation(pair + 1, 1 - pr)
            deviation(0, 0)
            weight_sums(0, 0, 16)
            turn(0, first=True)
            with act.Fori(1, PAIRS // 2 - 1) as i:
                turn(i)
            turn(PAIRS // 2 - 1, last=True)

            a.activation(gelu_b, b1t[:, :], ACT.Gelu).then_inc(s["gelu_ok"], 1)
            act.wait_ge(s["z_ok"], 1)
            a.activation(small[:, 20:21], small[:, 19:20], ACT.Exp, scale=-1.0).then_inc(s["exp_ok"], 1)

            bias, total, above, shift = [search[:, n:n + 1] for n in range(4)]
            chain = [0]

            def then(ins):
                chain[0] += 1
                ins.then_inc(s["search"], 1)
                act.wait_ge(s["search"], chain[0])

            def find(keys, digits, found):
                for n in range(digits):
                    then(a.activation(signs, keys, ACT.Sign, bias=bias, accum_out=total))
                    then(a.activation(above, total, ACT.Sign, bias=shift))
                    last = a.activation(bias, above, ACT.Identity, scale=-(2.0 ** (digits - 2 - n)), bias=bias)
                    if n < digits - 1:
                        then(last)
                last.then_inc(found, 1)
            act.wait_ge(s["key_hi_ok"], 1)
            find(key_hi, 14, s["hi_found"])
            act.wait_ge(s["key_lo_ok"], 1)
            find(key_hi, 16, s["lo_found"])

            def split_x(j, p):
                act.wait_ge(s["f_xt"], j + 1)
                if not (isinstance(j, int) and j < 2):
                    act.wait_ge(s["f_h"], (j - 1) * 4)
                a.activation(xhi[p].rearrange("p k t -> p (k t)"), ps_x[p][:, 0:K * W], ACT.Copy,
                             scale=XS).then_inc(s["f_xhi"], 1)

            def hidden(j):
                e = act.value_load(tile_expert[0:1, bass.ds(j, 1)], min_val=0, max_val=E - 1)
                for qt in range(4):
                    act.wait_ge(s["f_h"], j * 4 + (1 + qt))
                    if not (isinstance(j, int) and j < 1):
                        act.wait_ge(s["f_hlo"], (j - 1) * 4 + (1 + qt))
                    for c in range(qt * CQ, (qt + 1) * CQ):
                        ins = a.activation(h32[:, c * W:(c + 1) * W], ps_h[qt][:, c % CQ * W:(c % CQ + 1) * W], ACT.Gelu,
                                           bias=b1t[:, bass.ds(e * C + c, 1)], scale=inv_in[:, bass.ds(e, 1)])
                    ins.then_inc(s["f_gelu"], 1)
            act.wait_ge(s["idx_ok"], 1)

            def step(j, p):
                split_x(j + 1, 1 - p)
                hidden(j)
            split_x(0, 0)
            for j in range(PEEL):
                step(j, j % 2)
            with act.Fori(PEEL // 2, NT // 2) as i:
                for p in range(2):
                    step(i * 2 + p, p)
            hidden(NT - 1)

        @block.tensor
        def _(pe):
            t = nc.tensor
            pe.wait_ge(s["params_in"], PARAMS)
            pe.wait_ge(s["consts"], 1)
            for k in range(K):
                t.transpose(ps_s[:, k * N:(k + 1) * N], st_b[:, k * P:(k + 1) * P], ident[0:N, 0:N])
            t.transpose(ps_s[:, 128 + 0:128 + P], st_c[:, 0, :, :].rearrange("p r n -> p (r n)"), ident[:])
            last = t.transpose(ps_s[:, 128 + P:128 + 2 * P], st_c[:, 1, :, :].rearrange("p r n -> p (r n)"), ident[:])
            last.then_inc(s["pe_const"], 1)
            for k in range(K):
                last = t.transpose(ps_s[:, 384 + k * E:384 + (k + 1) * E], st_w[:, k * P:(k + 1) * P], ident[0:E, 0:E])
            last.then_inc(s["pe_const"], 1)
            t.transpose(ps_g[:, 64:64 + E * C], st_b1, ident[0:E * C, 0:E * C]).then_inc(s["pe_const"], 1)
            t.matmul(ps_g[:, 128:128 + D], ones[0:E, :], st_b2, start=True, stop=True).then_inc(s["pe_const"], 1)
            pe.wait_ge(s["dve_const"], 1)
            for k in range(K):
                last = t.matmul(ps_g[:, 0:E], ones[:], watsq[:, k * E:(k + 1) * E], start=(k == 0), stop=(k == K - 1))
            last.then_inc(s["pe_const"], 1)

            def turn(i):
                for pr in range(2):
                    pair = i * 2 + pr
                    for h in range(2):
                        bat = i * 4 + (2 * pr + h)
                        pe.wait_ge(s["xn_ok"], bat + 1)
                        for k in range(K):
                            if not (isinstance(i, int) and i == 0 and pr == 0 and h == 0):
                                pe.wait_ge(s["xt_out"], bat * K + (k + 1 - K))
                            for q in range(Q):
                                last = t.transpose(ps_t[:, k * S + q * P:k * S + (q + 1) * P],
                                                   xnb[h][:, q, k * P:(k + 1) * P], ident[:])
                            last.then_inc(s["xt_ok"], 1)
                    for h in range(2):
                        bat = i * 4 + (2 * pr + h)
                        pe.wait_ge(s["xt_out"], bat * K + K)
                        if not (isinstance(i, int) and i == 0 and pr == 0):
                            pe.wait_ge(s["scan_ok"], bat - 1)
                            pe.wait_ge(s["num_ok"], bat - 1)
                        for k in range(K):
                            last = t.matmul(bu_bank[h][0:NE, :], bwk[:, k, :], xnt[h][:, k, :],
                                            start=(k == 0), stop=(k == K - 1))
                        last.then_inc(s["bu_ok"], 1)
                    for h in range(2):
                        bat = i * 4 + (2 * pr + h)
                        if not (isinstance(i, int) and i == 0 and pr == 0):
                            pe.wait_ge(s["base_ok"], bat - 1)
                        pe.wait_ge(s["scan_ok"], bat + 1)
                        for q in range(Q):
                            last = t.matmul(y_bank(h, q), hs[h][0:N, q * P:(q + 1) * P], ct[0:N, :],
                                            start=True, stop=True)
                        last.then_inc(s["y_ok"], 1)
            pe.wait_ge(s["dve_const"], 2)
            turn(0)
            with pe.Fori(1, PAIRS // 2) as i:
                turn(i)

            pe.wait_ge(s["num_back"], 16)
            pe.wait_ge(s["scan_ok"], B)
            pe.wait_ge(s["num_ok"], B)
            for q in range(Q):
                last = t.transpose(ps_num[:, q * P:(q + 1) * P], num_rows[:, q * P:(q + 1) * P], ident[:])
            last.then_inc(s["num_t"], 1)

            def masked(e):
                for c in range(C):
                    n = e * C + c
                    w2h = whi[:, (2 * e + 1) * UW + c * D:(2 * e + 1) * UW + (c + 1) * D]
                    w2l = wlo[:, (2 * e + 1) * UW + c * D:(2 * e + 1) * UW + (c + 1) * D]
                    gh = gb16[:, n:n + 1].to_broadcast([P, P])
                    gl = gb16[:, E * C + n:E * C + n + 1].to_broadcast([P, P])
                    t.matmul(g_bank(e), gh, w2h, start=(c == 0), stop=False)
                    t.matmul(g_bank(e), gh, w2l, start=False, stop=False)
                    last = t.matmul(g_bank(e), gl, w2h, start=False, stop=(c == C - 1))
                last.then_inc(s["g_pe"], 1)
            pe.wait_ge(s["aff_ok"], 1)
            for q in range(Q):
                t.transpose(ps_t[:, q * P:(q + 1) * P], aff[:, q * P:(q + 1) * P], ident[:])
            t.matmul(ps_t[:, S:S + 1], ones[:], small[:, 16:17], start=True, stop=True).then_inc(s["aff_t"], 1)
            pe.wait_ge(s["gb_ok"], 1)
            pe.wait_ge(s["base_ok"], B)
            masked(0)
            pe.wait_ge(s["oh_ok"], 1)
            pe.wait_ge(s["tri_ok"], 1)
            t.matmul(ps_s[:, 0:TE], tri16, oh16, start=True, stop=True)
            t.matmul(ps_bu[:, 0:TE], ones16, oh16, start=True, stop=True).then_inc(s["counts_ok"], 1)
            for e in range(1, E):
                masked(e)
            for tt in range(T):
                if tt % (T // 4) == 0:
                    pe.wait_ge(s["planes_ok"], 1 + tt // (T // 4))
                    pe.wait_ge(s["tile_no_ok"], 1 + tt // (T // 4))
                last = t.matmul(ps_s[:, 0:2 * NS], lo16[:, tt, :], v16[:, :, tt, :], start=(tt == 0), stop=(tt == T - 1))
            last.then_inc(s["inverse_ok"], 1)

            def kept_tokens():
                pe.wait_ge(s["kept_ok"], 1)
                for q in range(Q):
                    last = t.transpose(ps_num[:, q * P:(q + 1) * P], eq_rows[:, q * P:(q + 1) * P], ident[:])
                last.then_inc(s["kept_t"], 1)

            def kept_slots():
                pe.wait_ge(s["kept_e_ok"], 1)
                for tt in range(T):
                    last = t.matmul(ps_num[:, 0:NS], lo16[:, tt, :], e16[:, tt, :], start=(tt == 0), stop=(tt == T - 1))
                last.then_inc(s["kept_inv"], 1)
                pe.wait_ge(s["mask_ok"], 1)

            gx = [s["gx0"], s["gx1"]]

            def rows_t(j, p, k):
                pe.wait_ge(gx[p], k * 32 + 32)
                if not (isinstance(j, int) and j < 2):
                    pe.wait_ge(s["f_xlo"], j - 1)
                for kk in range(K):
                    for h in range(2):
                        last = t.transpose(ps_x[p][:, kk * W + h * P:kk * W + (h + 1) * P],
                                           xg[p][:, h * D + kk * P:h * D + (kk + 1) * P], ident[:])
                last.then_inc(s["f_xt"], 1)

            def up(j, p):
                e = pe.value_load(tile_expert[0:1, bass.ds(j, 1)], min_val=0, max_val=E - 1)
                w0 = pe.snap(e * (2 * UW))
                pe.wait_ge(s["f_xlo"], j + 1)
                for qt in range(4):
                    if not (isinstance(j, int) and j < 1):
                        pe.wait_ge(s["f_gelu"], (j - 1) * 4 + (1 + qt))
                    for c in range(qt * CQ, (qt + 1) * CQ):
                        dst = ps_h[qt][:, c % CQ * W:(c % CQ + 1) * W]
                        for k in range(K):
                            wh = whi[:, bass.ds(w0 + (k * F + c * P), P)]
                            wl = wlo[:, bass.ds(w0 + (k * F + c * P), P)]
                            t.matmul(dst, wh, xhi[p][:, k, :], start=(k == 0), stop=False)
                            t.matmul(dst, wh, xlo[p][:, k, :], start=False, stop=False)
                            last = t.matmul(dst, wl, xhi[p][:, k, :], start=False, stop=(k == K - 1))
                    last.then_inc(s["f_h"], 1)

            def down(j, p):
                e = pe.value_load(tile_expert[0:1, bass.ds(j, 1)], min_val=0, max_val=E - 1)
                w0 = pe.snap(e * (2 * UW) + UW)
                if not (isinstance(j, int) and j < 2):
                    pe.wait_ge(s["f_yr"], j - 1)
                for h in range(2):
                    for c in range(C):
                        if h == 0 and c % CQ == 0:
                            pe.wait_ge(s["f_hlo"], j * 4 + (1 + c // CQ))
                        wh = whi[:, bass.ds(w0 + c * D, D)]
                        wl = wlo[:, bass.ds(w0 + c * D, D)]
                        dst = ps_o[p][:, h * D:(h + 1) * D]
                        hh = hhi[p][:, c * W + h * P:c * W + (h + 1) * P]
                        hl = hlo[p][:, c * W + h * P:c * W + (h + 1) * P]
                        t.matmul(dst, hh, wh, start=(c == 0), stop=False)
                        t.matmul(dst, hh, wl, start=False, stop=False)
                        last = t.matmul(dst, hl, wh, start=False, stop=(c == C - 1))
                last.then_inc(s["f_y"], 1)
            pe.wait_ge(s["idx_ok"], 1)
            pe.wait_ge(s["g_out"], E)

            def step(j, p, k):
                rows_t(j + 1, 1 - p, k + p)
                up(j, p)
                if isinstance(j, int) and j == 0:
                    kept_tokens()
                else:
                    down(j - 1, 1 - p)
                if isinstance(j, int) and j == 1:
                    kept_slots()
            rows_t(0, 0, 0)
            for j in range(PEEL):
                step(j, j % 2, j // 2)
            with pe.Fori(PEEL // 2, NT // 2) as i:
                for p in range(2):
                    step(i * 2 + p, p, i)
            up(NT - 1, 0)
            down(NT - 2, 1)
            down(NT - 1, 0)

        @block.vector
        def _(dve):
            v = nc.vector
            link_n = [0]

            def link(ins):
                link_n[0] += 1
                ins.then_inc(s["dve_chain"], 1)
                dve.wait_ge(s["dve_chain"], link_n[0])

            def power_of_two(dst, src, n, exps):
                link(v.tensor_scalar(exps, src.bitcast(I32), 23, None, ALU.logical_shift_right))
                link(v.tensor_scalar(exps, exps, -1.0, 268.0, ALU.mult, ALU.add))
                link(v.tensor_scalar(exps, exps, 250.0, 4.0, ALU.min, ALU.max))
                link(v.tensor_scalar(dst.bitcast(I32), exps, 23, None, ALU.logical_shift_left))

            def stats_of(pair, nb, first, between=lambda h: None):
                pr = nb // 2
                for h in range(2):
                    n = nb + h
                    if isinstance(pair, int):
                        dve.wait_ge(x_in[n], 16 * (pair // 2 + 1))
                    else:
                        dve.wait_ge(x_in[n], first)
                    for q in range(Q):
                        c = (h * Q + q) * 6
                        last = v.bn_stats(stats[:, c:c + 6], xb[n][:, q, :])
                    if h == 1:
                        last.then_inc(s["r_dve2"], 1)
                    between(h)
                dve.wait_ge(s["r_dve2"], pair * 2 + 1)
                v.memset(cnt[:, 4:5], 0.0)
                for c in range(2 * Q):
                    last = v.bn_aggr(mv[pr][:, 2 * c:2 * c + 2], stats[:, c * 6:(c + 1) * 6])
                last.then_inc(s["r_dve2"], 1)
                dve.wait_ge(s["r_dve2"], pair * 2 + 2)
                v.tensor_scalar(ve[pr], mv[pr].rearrange("p (t m) -> p t m", m=2)[:, :, 1],
                                EPS, None, ALU.add).then_inc(s["stats"], 1)

            def rstd_of(pair, pr, between=lambda n: None):
                r_ = rstd[pr]
                v_ = ve[pr]
                nw = s["newton"]
                dve.wait_ge(s["std"], pair + 1)
                v.reciprocal(r_, r_).then_inc(nw, 1)
                between(0)
                dve.wait_ge(nw, pair * 5 + 1)
                v.tensor_tensor(newt[:, :], r_, r_, ALU.mult).then_inc(nw, 1)
                between(1)
                dve.wait_ge(nw, pair * 5 + 2)
                v.tensor_tensor(newt[:, :], newt[:, :], v_, ALU.mult).then_inc(nw, 1)
                between(2)
                dve.wait_ge(nw, pair * 5 + 3)
                v.tensor_scalar(newt[:, :], newt[:, :], -0.5, 1.5, ALU.mult, ALU.add).then_inc(nw, 1)
                between(3)
                dve.wait_ge(nw, pair * 5 + 4)
                v.tensor_tensor(r_, r_, newt[:, :], ALU.mult).then_inc(nw, 1)
                dve.wait_ge(nw, pair * 5 + 5)
                v.tensor_tensor(newt[:, :], mv[pr].rearrange("p (t m) -> p t m", m=2)[:, :, 1], r_,
                                ALU.mult).then_inc(s["ratio_c"], 1)
                dve.wait_ge(s["ratio_c"], pair + 1)
                v.tensor_tensor(ratio_all[:, bass.ds(pair * (2 * Q), 2 * Q)], newt[:, :], r_,
                                ALU.mult).then_inc(s["ratios_ok"], 1)

            def weight_scales(pair, pr, steps=False):
                ws = s["wchain"]
                ex = exp_w[:, bass.ds(pair * 2, 2)]

                def step(n):
                    if n == 0:
                        dve.wait_ge(s["wmax_ok"], pair * 2 + 2)
                        v.tensor_scalar(ex, wmax[:, 2 * pr:2 * pr + 2].bitcast(I32), 23, None,
                                        ALU.logical_shift_right).then_inc(ws, 1)
                        return
                    dve.wait_ge(ws, pair * 3 + n)
                    if n == 1:
                        v.tensor_scalar(ex, ex, -1.0, 268.0, ALU.mult, ALU.add).then_inc(ws, 1)
                    elif n == 2:
                        v.tensor_scalar(ex, ex, 250.0, 4.0, ALU.min, ALU.max).then_inc(ws, 1)
                    else:
                        v.tensor_scalar(scale_w[:, bass.ds(pair * 2, 2)].bitcast(I32), ex, 23, None,
                                        ALU.logical_shift_left).then_inc(s["wscale_ok"], 1)
                if steps:
                    return step
                for n in range(4):
                    step(n)

            def low_part(pair, pr, w):
                uu = pair * 2 + w
                dve.wait_ge(s["whi_ok"], uu + 1)
                v.scalar_tensor_tensor(out=wlo[:, bass.ds(uu * UW, UW)], in0=raw[2 * pr + w],
                                       scalar=scale_w[:, bass.ds(uu, 1)], in1=whi[:, bass.ds(uu * UW, UW)],
                                       op0=ALU.mult, op1=ALU.subtract).then_inc(s["wlo_ok"], 1)

            def add_y(bat, n):
                dve.wait_ge(s["y_ok"], bat + 1)
                dve.wait_ge(s["dx_ok"], bat * 2 + 2)
                xf = xb[n].rearrange("p q d -> p (q d)")
                if n % 2 == 0:
                    v.tensor_tensor(xf, ps_y[:, :], xf, ALU.add).then_inc(s["base_ok"], 1)
                else:
                    v.tensor_tensor(xf[:, 0:2 * D], ps_s[:, 0:2 * D], xf[:, 0:2 * D], ALU.add)
                    v.tensor_tensor(xf[:, 2 * D:4 * D], ps_g[:, 0:2 * D], xf[:, 2 * D:4 * D],
                                    ALU.add).then_inc(s["base_ok"], 1)

            def te(x):
                return x.rearrange("p (t e) -> p t e", e=E)
            def bt_(x):
                return x.rearrange("p (t a) -> p t a", a=1).to_broadcast([P, T, E])
            def be_(x):
                return x.rearrange("p (a e) -> p a e", a=1).to_broadcast([P, T, E])

            def square_norms():
                dve.wait_ge(s["ratios_ok"], PAIRS)
                v.tensor_copy(xnorm.rearrange("p (q b) -> p q b", q=Q),
                              ratio_all[:, :].rearrange("p (b q) -> p q b", q=Q)).then_inc(s["xnorm_ok"], 1)

            def norms():
                dve.wait_ge(s["xroot_ok"], 1)
                link(v.tensor_scalar(sq1, sq0, 1e-30, None, ALU.max))
                link(v.reciprocal(ratio, sq1))
                link(v.tensor_tensor(sq1, ratio, xnorm, ALU.mult))
                link(v.tensor_tensor(ratio, sq1, sq0, ALU.add))
                link(v.tensor_scalar(xnorm, ratio, 0.5 * float(D) ** 0.5, None, ALU.mult))

            def denominators():
                link(v.tensor_tensor(te(den), bt_(xnorm), be_(wnorm[:, :]), ALU.mult))
                link(v.tensor_scalar(den, den, 1e-9, None, ALU.add))

            def turn(i, first=False, last=False):
                for pr in range(2):
                    pair = i * 2 + pr
                    if last and pr == 1:
                        square_norms()
                    for h in range(2):
                        n = 2 * pr + h
                        bat = i * 4 + n
                        if not (first and pr == 0):
                            dve.wait_ge(s["xt_ok"], (bat - 1) * K)
                            dve.wait_ge(s["dx_ok"], (bat - 2) * 2 + 1)
                            dve.wait_ge(xn_out[h], pair * 16)
                        for q in range(Q):
                            tt = h * Q + q
                            ins = v.tensor_scalar(xnb[h][:, q, :], xb[n][:, q, :], mv[pr][:, 2 * tt:2 * tt + 1],
                                                  rstd[pr][:, tt:tt + 1], ALU.subtract, ALU.mult)
                        ins.then_inc(s["xn_ok"], 1)
                    if not (first and pr == 0):
                        low_part(pair, pr, 0)
                        low_part(pair, pr, 1)
                    def states(h):
                        dve.wait_ge(s["bu_ok"], i * 4 + (2 * pr + h + 1))
                        v.tensor_tensor_scan(hs[h][0:N, :], lam_c[0:N, :].to_broadcast([N, S]), bu_bank[h][0:N, :], 0.0,
                                             ALU.mult, ALU.add).then_inc(s["scan_ok"], 1)
                    if first and pr == 0:
                        weight_scales(0, 0)
                    if last and pr == 1:
                        norms()
                        states(0)
                        denominators()
                        states(1)
                        link(v.reciprocal(rden, den))
                    else:
                        stats_of(pair + 1, 2 * (1 - pr), i * 16 + 16 * (1 + pr), states)
                    if first and pr == 0:
                        low_part(0, 0, 0)
                        low_part(0, 0, 1)
                    for h in range(2):
                        add_y(i * 4 + (2 * pr + h), 2 * pr + h)
                    if not (last and pr == 1):
                        rstd_of(pair + 1, 1 - pr, weight_scales(pair + 1, 1 - pr, steps=True))
            stats_of(0, 0, None)
            dve.wait_ge(s["pe_const"], 2)
            v.tensor_copy(bwk[:, :, 0:N], ps_s[:, 0:K * N].rearrange("p (k n) -> p k n", k=K))
            v.tensor_copy(ct[:, :], ps_s[:, 128:128 + D])
            link(v.tensor_copy(bwk[:, :, N:NE], ps_s[:, 384:384 + K * E].rearrange("p (k n) -> p k n", k=K)))
            v.tensor_tensor(watsq.rearrange("p (k n) -> p k n", k=K), bwk[:, :, N:NE], bwk[:, :, N:NE], ALU.mult).then_inc(s["dve_const"], 1)
            dve.wait_ge(s["pe_const"], 5)
            dve.wait_ge(s["act_const"], 1)
            link(v.tensor_scalar(lam[:, 2:3], lam[:, 1:2], 1.0, None, ALU.add))
            link(v.reciprocal(lam[:, 3:4], lam[:, 2:3]))
            dve.wait_ge(s["act_const"], 2)
            v.tensor_copy(b1t[:, :], ps_g[:, 64:64 + E * C])
            v.tensor_copy(c_bc[:, :], ps_g[:, 128:128 + D])
            link(v.tensor_scalar(small[:, 8:16], small[:, 0:8], 1e-30, None, ALU.max))
            link(v.reciprocal(small[:, 24:32], small[:, 8:16]))
            link(v.tensor_tensor(small[:, 32:40], small[:, 24:32], ps_g[:, 0:E], ALU.mult))
            link(v.tensor_tensor(small[:, 8:16], small[:, 0:8], small[:, 32:40], ALU.add))
            link(v.tensor_scalar(wnorm[:, :], small[:, 8:16], 0.5, None, ALU.mult))
            v.memset(cnt[:, 0:1], 0.0).then_inc(s["dve_const"], 1)
            dve.wait_ge(s["dve_const"], 2)
            v.tensor_reduce(small[:, 48:56], b1t[:, :].rearrange("p (e c) -> p e c", c=C), AX.X, ALU.max,
                            apply_absolute_value=True).then_inc(s["b1_max"], 1)

            rstd_of(0, 0)
            turn(0, first=True)
            with dve.Fori(1, PAIRS // 2 - 1) as i:
                turn(i)
            turn(PAIRS // 2 - 1, last=True)
            for n in range(2):
                dve.wait_ge(base_out[n], 16 * (B // 4))
            dve.wait_ge(s["num_t"], 1)
            link(v.tensor_tensor(aff, ps_num[:, 0:TE], rden, ALU.mult))
            v.tensor_reduce(small[:, 16:17], aff, AX.X, ALU.add).then_inc(s["aff_ok"], 1)

            dve.wait_ge(s["aff_t"], 1)
            z, cap = small[:, 19:20], small[:, 21:22]
            link(v.tensor_scalar(small[:, 18:19], ps_t[:, S:S + 1], 1.0 / (TOKENS * E), None, ALU.mult))
            v.tensor_tensor(z, small[:, 18:19], thr_bc[:, :], ALU.subtract).then_inc(s["z_ok"], 1)
            link(v.tensor_copy(a_rows, ps_t[:, 0:S]))
            link(v.tensor_scalar(eq_rows, a_rows, 0.0, 0.0, ALU.is_ge, ALU.add, accum_out=cnt[:, 2:3]))
            dve.wait_ge(s["exp_ok"], 1)
            link(v.tensor_scalar(small[:, 17:18], small[:, 20:21], 1.0, None, ALU.add))
            link(v.reciprocal(small[:, 18:19], small[:, 17:18]))
            link(v.tensor_scalar(cap, small[:, 18:19], float(S), None, ALU.mult))
            link(v.tensor_copy(tmp_i[:, 0:1], cap))
            link(v.tensor_copy(small[:, 17:18], tmp_i[:, 0:1]))
            link(v.tensor_tensor(small[:, 18:19], small[:, 17:18], cap, ALU.is_gt))
            link(v.tensor_tensor(cap, small[:, 17:18], small[:, 18:19], ALU.subtract))
            link(v.tensor_scalar(cap, cap, 4.0, float(S), ALU.max, ALU.min))

            sign, kth, kneg = small[:, 22:23], small[:, 23:24], small[:, 17:18]
            link(v.tensor_tensor(kneg, cnt[:, 2:3], cap, ALU.is_lt))
            link(v.tensor_scalar(sign, kneg, -2.0, 1.0, ALU.mult, ALU.add))
            link(v.tensor_scalar(small[:, 18:19], cap, -2.0, float(S + 1), ALU.mult, ALU.add))
            link(v.scalar_tensor_tensor(out=kth, in0=small[:, 18:19], scalar=kneg, in1=cap, op0=ALU.mult, op1=ALU.add))
            v.tensor_scalar(search[:, 3:4], kth, -2.0, float(S + 1), ALU.mult, ALU.add)
            v.memset(search[:, 0:1], -(2.0 ** 13 - 0.5))
            link(v.tensor_scalar(eq_rows, a_rows, sign, 0.0, ALU.mult, ALU.add))
            key_i = rden.bitcast(I32)
            link(v.tensor_scalar(key_i, eq_rows.bitcast(I32), 16, None, ALU.arith_shift_right))
            v.tensor_copy(key_hi, key_i).then_inc(s["key_hi_ok"], 1)
            dve.wait_ge(s["key_hi_ok"], 1)
            link(v.tensor_scalar(key_i, eq_rows.bitcast(I32), 0xFFFF, None, ALU.bitwise_and))
            v.tensor_copy(eq_rows, key_i)
            low_half = eq_rows

            dve.wait_ge(s["b1_bound"], 1)
            ew = exp_w[:, :].rearrange("p (e w) -> p e w", w=2)
            link(v.tensor_scalar(tmp_i[:, 0:E], ew[:, :, 0], -1.0, 254.0 - 11.0, ALU.mult, ALU.add))
            link(v.tensor_scalar(tmp_i[:, 0:E], tmp_i[:, 0:E], 1.0, None, ALU.max))
            link(v.tensor_scalar(inv_in[:, :].bitcast(I32), tmp_i[:, 0:E], 23, None, ALU.logical_shift_left))
            link(v.scalar_tensor_tensor(out=small[:, 48:56], in0=inv_in[:, :], scalar=float(D) * 2.0 ** 15 * XS,
                                        in1=small[:, 56:64], op0=ALU.mult, op1=ALU.add))
            power_of_two(h_scale[:, :], small[:, 48:56], E, exp_h[:, :])
            link(v.scalar_tensor_tensor(out=tmp_i[:, 0:E], in0=ew[:, :, 1], scalar=-1.0, in1=exp_h[:, :],
                                        op0=ALU.mult, op1=ALU.subtract))
            link(v.tensor_scalar(tmp_i[:, 0:E], tmp_i[:, 0:E], 381.0, None, ALU.add))
            link(v.tensor_scalar(tmp_i[:, 0:E], tmp_i[:, 0:E], 1.0, 254.0, ALU.max, ALU.min))
            link(v.tensor_scalar(inv_out[:, :].bitcast(I32), tmp_i[:, 0:E], 23, None, ALU.logical_shift_left))
            dve.wait_ge(s["gelu_ok"], 1)
            gv = gelu_b.rearrange("p (e c) -> p e c", c=C)
            hb = h_scale[:, :].rearrange("p (e a) -> p e a", a=1).to_broadcast([P, E, C])
            link(v.tensor_tensor(gv, gv, hb, ALU.mult))
            link(v.tensor_copy(gb16[:, 0:E * C], gelu_b))
            v.tensor_tensor(gb16[:, E * C:2 * E * C], gelu_b, gb16[:, 0:E * C], ALU.subtract).then_inc(s["gb_ok"], 1)

            for n in range(4):
                dve.wait_ge(base_out[n], 16 * (B // 4))
            for n in range(2):
                dve.wait_ge(xn_out[n], 16 * (B // 2))
            link(v.tensor_reduce(rowmax, te(aff), AX.X, ALU.max))
            link(v.tensor_tensor(te(den), te(aff), bt_(rowmax), ALU.subtract))
            link(v.tensor_scalar(small[:, 40:48], iota_f[:, 0:E], -1.0, float(E), ALU.mult, ALU.add))
            link(v.scalar_tensor_tensor(out=te(rden), in0=te(den), scalar=NEAR, in1=be_(small[:, 40:48]),
                                        op0=ALU.is_ge, op1=ALU.mult))
            link(v.tensor_reduce(best, te(rden), AX.X, ALU.max))
            v.tensor_tensor(te(oh16), be_(small[:, 40:48]), bt_(best), ALU.is_equal).then_inc(s["oh_ok"], 1)

            dve.wait_ge(s["counts_ok"], 1)
            link(v.tensor_copy(cnt_e.rearrange("p (e t) -> p t e", e=E), te(ps_bu[:, 0:TE])))
            link(v.tensor_tensor_scan(scan_e, ones[:, 0:1].to_broadcast([P, TE]), cnt_e, 0.0, ALU.mult, ALU.add))
            n_e, end_e, t_incl, adj = small[:, 0:8], small[:, 8:16], small[:, 24:32], small[:, 32:40]
            tiles_e = small[:, 40:48]
            link(v.tensor_copy(end_e, scan_e.rearrange("p (e t) -> p e t", e=E)[:, :, T - 1]))
            v.tensor_copy(n_e[:, 0:1], end_e[:, 0:1])
            link(v.tensor_tensor(n_e[:, 1:E], end_e[:, 1:E], end_e[:, 0:E - 1], ALU.subtract))
            link(v.tensor_scalar(tiles_e, n_e, float(W - 1), None, ALU.add))
            link(v.tensor_copy(tmp_i[:, 0:E], tiles_e))
            link(v.tensor_scalar(tmp_i[:, 0:E], tmp_i[:, 0:E], W.bit_length() - 1, None, ALU.logical_shift_right))
            link(v.tensor_copy(tiles_e, tmp_i[:, 0:E]))
            link(v.tensor_tensor_scan(t_incl, ones[:, 0:E], tiles_e, 0.0, ALU.mult, ALU.add))
            link(v.tensor_tensor(adj, t_incl, tiles_e, ALU.subtract))
            link(v.tensor_tensor(end_e, end_e, n_e, ALU.subtract))
            link(v.scalar_tensor_tensor(out=adj, in0=adj, scalar=float(W), in1=end_e, op0=ALU.mult, op1=ALU.subtract))
            link(v.tensor_tensor(scan_e.rearrange("p (e t) -> p e t", e=E), scan_e.rearrange("p (e t) -> p e t", e=E),
                                 adj.rearrange("p (e a) -> p e a", a=1).to_broadcast([P, E, T]), ALU.add))
            link(v.tensor_tensor(te(pos4), te(ps_s[:, 0:TE]), scan_e.rearrange("p (e t) -> p t e", e=E), ALU.add))
            link(v.tensor_tensor(pos4, pos4, oh16, ALU.mult))
            link(v.tensor_reduce(pos, te(pos4), AX.X, ALU.add))
            link(v.tensor_copy(pos_i, pos))
            v.tensor_scalar(hi_i, pos_i, 7, None, ALU.logical_shift_right)
            link(v.tensor_scalar(lo_i, pos_i, P - 1, None, ALU.bitwise_and))
            v.tensor_copy(hi_f, hi_i)
            link(v.tensor_copy(lo_f, lo_i))
            def half_tile(half):
                ts = slice(half * T // 2, (half + 1) * T // 2)
                v.tensor_tensor(e16[:, ts, :], iota_f[:, 0:NS].rearrange("p (a j) -> p a j", a=1).to_broadcast([P, T // 2, NS]),
                                hi_f[:, ts].rearrange("p (t a) -> p t a", a=1).to_broadcast([P, T // 2, NS]),
                                ALU.is_equal).then_inc(s["e_ok"], 1)

            def place(quarter):
                ts = slice(quarter * T // 4, (quarter + 1) * T // 4)
                v.tensor_tensor(lo16[:, ts, :], iota_f[:, :].rearrange("p (a l) -> p a l", a=1).to_broadcast([P, T // 4, P]),
                                lo_f[:, ts].rearrange("p (t a) -> p t a", a=1).to_broadcast([P, T // 4, P]),
                                ALU.is_equal).then_inc(s["planes_ok"], 1)
            half_tile(0)
            dve.wait_ge(s["hi_found"], 1)
            v.tensor_scalar(search[:, 4:5], search[:, 0:1], -1.0, None, ALU.mult)
            link(v.tensor_scalar(key_hi, key_hi, search[:, 0:1], 2.0 ** 17, ALU.add, ALU.mult))
            v.memset(search[:, 0:1], -(2.0 ** 15 - 0.5))
            v.tensor_tensor(key_hi, key_hi, low_half, ALU.add).then_inc(s["key_lo_ok"], 1)
            half_tile(1)
            dve.wait_ge(s["e_ok"], 2)
            link(v.tensor_scalar(v16[:, 0], e16, pcol[:, 0:1], None, ALU.mult))
            for quarter in range(4):
                place(quarter)
            tc = tcmp.rearrange("p (j e) -> p j e", e=E)
            link(v.tensor_tensor(tc, iota_f[:, 0:NT].rearrange("p (j a) -> p j a", a=1).to_broadcast([P, NT, E]),
                                 t_incl.rearrange("p (a e) -> p a e", a=1).to_broadcast([P, NT, E]), ALU.is_ge))
            te_f = mask_slot[:, 0:NT]
            link(v.tensor_reduce(te_f, tc, AX.X, ALU.add))
            link(v.tensor_scalar(te_f, te_f, float(E - 1), None, ALU.min))
            link(v.tensor_copy(tile_expert, te_f))
            dve.wait_ge(s["inverse_ok"], 1)
            iv = mask_slot
            link(v.tensor_scalar(iv, ps_s[:, 0:NS], 0.5, float(4 * TOKENS), ALU.is_lt, ALU.mult))
            link(v.tensor_tensor(iv, ps_s[:, 0:NS], iv, ALU.add))
            link(v.scalar_tensor_tensor(out=iv, in0=ps_s[:, NS:2 * NS], scalar=float(P), in1=iv, op0=ALU.mult, op1=ALU.add))
            link(v.tensor_scalar(iv, iv, -1.0, None, ALU.add))
            v.tensor_copy(idx_all, iv).then_inc(s["idx_ok"], 1)
            for e in range(E):
                if e % 2 == 0:
                    dve.wait_ge(s["g_pe"], e + 2)
                v.tensor_scalar(g_bc[:, e * D:(e + 1) * D], g_bank(e), inv_out[:, e:e + 1], None,
                                ALU.mult).then_inc(s["g_out"], 1)

            def kept():
                dve.wait_ge(s["lo_found"], 1)
                thr = small[:, 26:27]
                v.tensor_copy(bits[:, 0:1], search[:, 4:5])
                link(v.tensor_scalar(search[:, 5:6], search[:, 0:1], -1.0, None, ALU.mult))
                link(v.tensor_copy(bits[:, 1:2], search[:, 5:6]))
                link(v.tensor_scalar(bits[:, 2:3], bits[:, 0:1], 16, None, ALU.logical_shift_left))
                link(v.tensor_tensor(bits[:, 3:4], bits[:, 2:3], bits[:, 1:2], ALU.bitwise_or))
                link(v.tensor_tensor(thr, bits[:, 3:4].bitcast(F32), sign, ALU.mult))
                gt = aff
                link(v.tensor_scalar(gt, a_rows, thr, 0.0, ALU.is_gt, ALU.add, accum_out=cnt[:, 3:4]))
                link(v.tensor_tensor(small[:, 27:28], cap, cnt[:, 3:4], ALU.subtract))
                link(v.tensor_scalar(eq_rows, a_rows, thr, None, ALU.is_equal))
                link(v.tensor_tensor_scan(a_rows, ones[:, 0:1].to_broadcast([P, S]), eq_rows, 0.0, ALU.mult, ALU.add))
                link(v.scalar_tensor_tensor(out=eq_rows, in0=a_rows, scalar=small[:, 27:28], in1=eq_rows,
                                            op0=ALU.is_le, op1=ALU.mult))
                v.tensor_tensor(eq_rows, eq_rows, gt, ALU.add).then_inc(s["kept_ok"], 1)

            def kept_half_tiles():
                dve.wait_ge(s["kept_t"], 1)
                link(v.tensor_tensor(aff, ps_num[:, 0:S], oh16, ALU.mult))
                v.tensor_reduce(mtok, te(aff), AX.X, ALU.add).then_inc(s["mtok_ok"], 1)

            def kept_by_slot():
                dve.wait_ge(s["kept_inv"], 1)
                v.tensor_copy(mask_slot, ps_num[:, 0:NS]).then_inc(s["mask_ok"], 1)

            def masked_sum():
                for e in range(E):
                    link(v.tensor_tensor(c_bc[:, :], c_bc[:, :], g_bc[:, e * D:(e + 1) * D], ALU.add))

            gb = [s["gb0"], s["gb1"]]
            sc = [s["sc0"], s["sc1"]]

            def x_low(j, p):
                dve.wait_ge(s["f_xhi"], j + 1)
                v.scalar_tensor_tensor(out=xlo[p].rearrange("p k t -> p (k t)"), in0=ps_x[p][:, 0:K * W], scalar=XS,
                                       in1=xhi[p].rearrange("p k t -> p (k t)"), op0=ALU.mult,
                                       op1=ALU.subtract).then_inc(s["f_xlo"], 1)

            def h_parts(j, p):
                e = dve.value_load(tile_expert[0:1, bass.ds(j, 1)], min_val=0, max_val=E - 1)
                for qt in range(4):
                    cs = slice(qt * QW, (qt + 1) * QW)
                    dve.wait_ge(s["f_gelu"], j * 4 + (1 + qt))
                    if qt == 0 and not (isinstance(j, int) and j < 2):
                        dve.wait_ge(s["f_y"], j - 1)
                    v.tensor_scalar(hhi[p][:, cs], h32[:, cs], h_scale[:, bass.ds(e, 1)], None,
                                    ALU.mult).then_inc(s["f_hhi"], 1)
                    dve.wait_ge(s["f_hhi"], j * 4 + (1 + qt))
                    v.scalar_tensor_tensor(out=hlo[p][:, cs], in0=h32[:, cs], scalar=h_scale[:, bass.ds(e, 1)],
                                           in1=hhi[p][:, cs], op0=ALU.mult, op1=ALU.subtract).then_inc(s["f_hlo"], 1)

            def result(j, p, k):
                e = dve.value_load(tile_expert[0:1, bass.ds(j, 1)], min_val=0, max_val=E - 1)
                dve.wait_ge(s["f_y"], j + 1)
                halves = [slice(h * D, (h + 1) * D) for h in range(2)]
                for hs_ in halves:
                    last = v.scalar_tensor_tensor(out=yr[p][:, hs_], in0=ps_o[p][:, hs_], scalar=inv_out[:, bass.ds(e, 1)],
                                                  in1=g_bc[:, bass.ds(e * D, D)], op0=ALU.mult, op1=ALU.subtract)
                last.then_inc(s["f_yr"], 1)
                dve.wait_ge(s["f_yr"], j + 1)
                dve.wait_ge(gb[p], k * 32 + 32)
                for h, hs_ in enumerate(halves):
                    last = v.scalar_tensor_tensor(out=yr[p][:, hs_], in0=yr[p][:, hs_],
                                                  scalar=mask_slot[:, bass.ds(j * 2 + h, 1)], in1=bg[p][:, hs_],
                                                  op0=ALU.mult, op1=ALU.add)
                last.then_inc(s["f_ym"], 1)
                dve.wait_ge(s["f_ym"], j + 1)
                if not (isinstance(k, int) and k == 0):
                    dve.wait_ge(sc[p], k * 32)
                v.tensor_tensor(og[p].rearrange("p (h d) -> p h d", h=2), yr[p].rearrange("p (h d) -> p h d", h=2),
                                c_bc[:, :].rearrange("p (a d) -> p a d", a=1).to_broadcast([P, 2, D]),
                                ALU.add).then_inc(s["f_o"], 1)

            def step(j, p, k):
                x_low(j + 1, 1 - p)
                if isinstance(j, int) and j == 0:
                    kept_half_tiles()
                if isinstance(j, int) and j == 1:
                    kept_by_slot()
                h_parts(j, p)
                if isinstance(j, int) and j == 1:
                    masked_sum()
                if not (isinstance(j, int) and j < 1):
                    result(j - 1, 1 - p, k - 1 + p)
            x_low(0, 0)
            kept()
            for j in range(PEEL):
                step(j, j % 2, j // 2)
            with dve.Fori(PEEL // 2, NT // 2) as i:
                for p in range(2):
                    step(i * 2 + p, p, i)
            h_parts(NT - 1, 0)
            result(NT - 2, 1, NT // 2 - 1)
            result(NT - 1, 0, NT // 2)


_INS = ["L0_attn_u", "L0_attn_log_lambda", "L0_attn_B_w", "L0_attn_C_w", "L0_attn_D", "L0_ffn_waff",
        "L0_ffn_W1", "L0_ffn_b1", "L0_ffn_W2", "L0_ffn_b2", "L0_ffn_affinity_threshold"]


def kernel(**inputs):
    import numpy as _np
    import concourse.bacc as _bacc
    from concourse.bass_utils import run_bass_kernel_spmd as _run

    nc = _bacc.Bacc("TRN2", target_bir_lowering=False, num_devices=1)
    arrays, args = {}, []
    for name in _INS:
        a = _np.ascontiguousarray(inputs[name])
        if a.ndim == 0:
            a = a.reshape(1)
        arrays[name] = a
        args.append(nc.dram_tensor(name, a.shape, F32, kind="ExternalInput").ap())
    shape = inputs["L0_attn_u"].shape
    out = nc.dram_tensor("out", shape, F32, kind="ExternalOutput").ap()
    rows = [shape[0] * shape[1], shape[2]]
    xn = nc.dram_tensor("xn_rows", rows, F32).ap()
    base = nc.dram_tensor("base_rows", rows, F32).ap()
    num = nc.dram_tensor("router_rows", [shape[0] * inputs["L0_ffn_waff"].shape[0], shape[1]], F32).ap()
    moe_ssm_kernel(nc, *args, out, xn, base, num)
    r = _run(nc, [arrays], core_ids=[0])
    return r.results[0]["out"]
```
